# Optimizing a Trainium2 kernel written in Bass

```python
import numpy as np
import jax
import jax.numpy as jnp

def _softmax(x, axis=-1):
    return jax.nn.softmax(x, axis=axis)

def _gelu(x):
    return jax.nn.gelu(x, approximate=True)

def _silu(x):
    return jax.nn.silu(x)

def _sigmoid(x):
    return jax.nn.sigmoid(x)

def _layernorm(x, axis=-1, eps=1e-05):
    m = jnp.mean(x, axis=axis, keepdims=True)
    v = jnp.var(x, axis=axis, keepdims=True)
    return (x - m) / jnp.sqrt(v + eps)

def _scatter_add(tgt, idx, src, axis=0):
    return tgt.at[idx].add(src)

def _segment_sum(src, seg, n):
    return jax.ops.segment_sum(src, seg, n)
kernel_name = 'mk_decoder_preln_d1_seqx_r8_5bd008'

def setup_inputs(seed: int=0):
    np.random.seed(seed)
    _w = jnp.asarray

    def _rec_inputs():
        import jax
        import jax.numpy as jnp
        _rk = jax.random.key(seed)
        x = 6.313e-05 + 0.9998 * jax.random.normal(jax.random.fold_in(_rk, 1), (2, 512, 128), jnp.float32)
        _lenS = 512 - jax.random.randint(jax.random.fold_in(_rk, 7), (2,), 0, max(1, 512 // 4) + 1, jnp.int32)
        _lenS2 = 77 - jax.random.randint(jax.random.fold_in(_rk, 8), (2,), 0, max(1, 77 // 4) + 1, jnp.int32)
        _ctx_1024P = jax.random.normal(jax.random.fold_in(_rk, 11), (2, 16, 128), jnp.float32)
        _ctx_1024c = jax.random.dirichlet(jax.random.fold_in(_rk, 511), 0.3 * jnp.ones((16,), jnp.float32), (2, 77))
        _ctx_1024t = jnp.einsum('bsk,bkd->bsd', _ctx_1024c, _ctx_1024P)
        _ctx_1024t = _ctx_1024t * jax.lax.rsqrt(jnp.mean(jnp.square(_ctx_1024t)) + 1e-12) * 0.953939
        ctx_1024 = -0.000214406 + 1.00034 * (_ctx_1024t + 0.3 * jax.random.normal(jax.random.fold_in(_rk, 611), (2, 77, 128), jnp.float32))
        return (x, ctx_1024)
    x, ctx_1024 = _rec_inputs()

    def _L0_attn_setup():
        import jax, jax.numpy as jnp
        import numpy as np
        T, B, E, H = (128, 8, 128, 16)
        DH = E // H
        MASKED_BIAS = -10000.0
        key = jax.random.key(seed)
        k1, k2, k3 = jax.random.split(key, 3)
        query = jax.random.normal(k1, (T, B, E), dtype=jnp.float32)
        qkv_w = jax.random.normal(k2, (3 * E, E), dtype=jnp.float32) * (1.0 / np.sqrt(2.0 * E))
        out_w = jax.random.normal(k3, (E, E), dtype=jnp.float32) * (1.0 / np.sqrt(E))
        return {'query': query, 'qkv_w': qkv_w, 'qkv_b': jnp.zeros((3 * E,), jnp.float32), 'out_w': out_w, 'out_b': jnp.zeros((E,), jnp.float32)}
    _L0_attn_all = _L0_attn_setup()
    _L0_attn_in = {k: v for k, v in _L0_attn_all.items() if k in ('qkv_w', 'qkv_b', 'out_w', 'out_b')}
    del _L0_attn_all

    def _L0_xattn_setup():
        import jax, jax.numpy as jnp
        import numpy as np
        from jax import lax
        BIG = jnp.float32(1e+30)

        def _pairwise_euclidean(a, b):
            aa = jnp.sum(a * a, axis=-1)[:, None]
            bb = jnp.sum(b * b, axis=-1)[None, :]
            ab = a @ b.T
            return jnp.sqrt(jnp.maximum(aa + bb - 2.0 * ab, 0.0))

        def _dtw_cost(D):
            row0 = jnp.cumsum(D[0])

            def row_step(prev_row, d_row):
                first = d_row[0] + prev_row[0]

                def col_step(left, inp):
                    d_ij, up, diag = inp
                    r = d_ij + jnp.minimum(jnp.minimum(up, left), diag)
                    return (r, r)
                _, rest = lax.scan(col_step, first, (d_row[1:], prev_row[1:], prev_row[:-1]))
                row = jnp.concatenate([first[None], rest])
                return (row, row)
            _, rows = lax.scan(row_step, row0, D[1:])
            return jnp.concatenate([row0[None], rows], axis=0)

        def _backtrack(R, T1, T2):
            L = T1 + T2 - 1

            def step(carry, _):
                i, j, done = carry
                valid = jnp.logical_not(done)
                cd = jnp.where((i > 0) & (j > 0), R[jnp.maximum(i - 1, 0), jnp.maximum(j - 1, 0)], BIG)
                cu = jnp.where(i > 0, R[jnp.maximum(i - 1, 0), j], BIG)
                cl = jnp.where(j > 0, R[i, jnp.maximum(j - 1, 0)], BIG)
                choice = jnp.argmin(jnp.stack([cd, cu, cl]))
                ni = jnp.where(choice <= 1, i - 1, i)
                nj = jnp.where((choice == 0) | (choice == 2), j - 1, j)
                at_origin = (i == 0) & (j == 0)
                ni = jnp.where(at_origin, 0, ni)
                nj = jnp.where(at_origin, 0, nj)
                return ((ni, nj, done | at_origin), (i, j, valid))
            init = (jnp.int32(T1 - 1), jnp.int32(T2 - 1), jnp.bool_(False))
            _, (i_idx, j_idx, valid) = lax.scan(step, init, None, length=L)
            return (i_idx, j_idx, valid)

        def _align_one(small, large):
            T_small, d = small.shape
            T_large = large.shape[0]
            D = _pairwise_euclidean(small, large)
            R = _dtw_cost(D)
            i_idx, j_idx, valid = _backtrack(R, T_small, T_large)
            contrib = small[i_idx] * valid[:, None].astype(small.dtype)
            expanded = jnp.zeros((T_large, d), dtype=small.dtype).at[j_idx].add(contrib)
            return expanded
        key = jax.random.key(seed)
        k1, k2 = jax.random.split(key)
        teacher = jax.random.normal(k1, (16, 50, 128), dtype=jnp.float32)
        student = jax.random.normal(k2, (16, 75, 128), dtype=jnp.float32)
        return {'teacher_features': teacher, 'student_features': student}
    _L0_xattn_all = _L0_xattn_setup()
    _L0_xattn_in = {k: v for k, v in _L0_xattn_all.items() if k in ()}
    del _L0_xattn_all

    def _L0_ffn_setup():
        import jax, jax.numpy as jnp
        import numpy as np
        B, S, D, E, K = (4, 256, 128, 8, 2)
        H = 4 * D
        key = jax.random.key(seed)
        ks = jax.random.split(key, 4)
        sc = lambda n: 1.0 / np.sqrt(n)
        return {'x': jax.random.normal(ks[0], (B, S, D), jnp.float32), 'gate_w': jax.random.normal(ks[1], (D, E), jnp.float32) * sc(D), 'gate_b': jnp.zeros((E,), jnp.float32), 'w1': jax.random.normal(ks[2], (E, D, H), jnp.float32) * sc(D), 'b1': jnp.zeros((E, H), jnp.float32), 'w2': jax.random.normal(ks[3], (E, H, D), jnp.float32) * sc(H), 'b2': jnp.zeros((E, D), jnp.float32)}
    _L0_ffn_all = _L0_ffn_setup()
    _L0_ffn_in = {k: v for k, v in _L0_ffn_all.items() if k in ('gate_w', 'gate_b', 'w1', 'b1', 'w2', 'b2')}
    del _L0_ffn_all
    return {'x': x, 'ctx_1024': ctx_1024, 'L0_attn_qkv_w': _L0_attn_in['qkv_w'], 'L0_attn_qkv_b': _L0_attn_in['qkv_b'], 'L0_attn_out_w': _L0_attn_in['out_w'], 'L0_attn_out_b': _L0_attn_in['out_b'], 'L0_ffn_gate_w': _L0_ffn_in['gate_w'], 'L0_ffn_gate_b': _L0_ffn_in['gate_b'], 'L0_ffn_w1': _L0_ffn_in['w1'], 'L0_ffn_b1': _L0_ffn_in['b1'], 'L0_ffn_w2': _L0_ffn_in['w2'], 'L0_ffn_b2': _L0_ffn_in['b2']}

def reference(x, ctx_1024, L0_attn_qkv_w, L0_attn_qkv_b, L0_attn_out_w, L0_attn_out_b, L0_ffn_gate_w, L0_ffn_gate_b, L0_ffn_w1, L0_ffn_b1, L0_ffn_w2, L0_ffn_b2):
    import jax
    import jax.numpy as jnp

    def _L0_attn_ref(query, qkv_w, qkv_b, out_w, out_b):
        import jax, jax.numpy as jnp
        import numpy as np
        T, B, E, H = (128, 8, 128, 16)
        DH = E // H
        MASKED_BIAS = -10000.0
        tgt_len, bsz, embed_dim = query.shape
        scaling = DH ** (-0.5)
        qkv = jnp.einsum('tbe,fe->tbf', query, qkv_w) + qkv_b
        q, k, v = jnp.split(qkv, 3, axis=-1)
        q = q * scaling

        def to_heads(x):
            return x.reshape(tgt_len, bsz * H, DH).transpose(1, 0, 2)
        q, k, v = (to_heads(q), to_heads(k), to_heads(v))
        attn_weights = jnp.einsum('ntd,nsd->nts', q, k)
        causal = jnp.tril(jnp.ones((tgt_len, tgt_len), dtype=bool))
        attn_weights = jnp.where(causal[None, :, :], attn_weights, jnp.asarray(MASKED_BIAS, attn_weights.dtype))
        attn_probs = jax.nn.softmax(attn_weights, axis=-1)
        attn = jnp.einsum('nts,nsd->ntd', attn_probs, v)
        attn = attn.transpose(1, 0, 2).reshape(tgt_len, bsz, embed_dim)
        out = jnp.einsum('tbe,fe->tbf', attn, out_w) + out_b
        return out

    def _L0_xattn_ref(teacher_features, student_features):
        import jax, jax.numpy as jnp
        import numpy as np
        from jax import lax
        BIG = jnp.float32(1e+30)

        def _pairwise_euclidean(a, b):
            aa = jnp.sum(a * a, axis=-1)[:, None]
            bb = jnp.sum(b * b, axis=-1)[None, :]
            ab = a @ b.T
            return jnp.sqrt(jnp.maximum(aa + bb - 2.0 * ab, 0.0))

        def _dtw_cost(D):
            row0 = jnp.cumsum(D[0])

            def row_step(prev_row, d_row):
                first = d_row[0] + prev_row[0]

                def col_step(left, inp):
                    d_ij, up, diag = inp
                    r = d_ij + jnp.minimum(jnp.minimum(up, left), diag)
                    return (r, r)
                _, rest = lax.scan(col_step, first, (d_row[1:], prev_row[1:], prev_row[:-1]))
                row = jnp.concatenate([first[None], rest])
                return (row, row)
            _, rows = lax.scan(row_step, row0, D[1:])
            return jnp.concatenate([row0[None], rows], axis=0)

        def _backtrack(R, T1, T2):
            L = T1 + T2 - 1

            def step(carry, _):
                i, j, done = carry
                valid = jnp.logical_not(done)
                cd = jnp.where((i > 0) & (j > 0), R[jnp.maximum(i - 1, 0), jnp.maximum(j - 1, 0)], BIG)
                cu = jnp.where(i > 0, R[jnp.maximum(i - 1, 0), j], BIG)
                cl = jnp.where(j > 0, R[i, jnp.maximum(j - 1, 0)], BIG)
                choice = jnp.argmin(jnp.stack([cd, cu, cl]))
                ni = jnp.where(choice <= 1, i - 1, i)
                nj = jnp.where((choice == 0) | (choice == 2), j - 1, j)
                at_origin = (i == 0) & (j == 0)
                ni = jnp.where(at_origin, 0, ni)
                nj = jnp.where(at_origin, 0, nj)
                return ((ni, nj, done | at_origin), (i, j, valid))
            init = (jnp.int32(T1 - 1), jnp.int32(T2 - 1), jnp.bool_(False))
            _, (i_idx, j_idx, valid) = lax.scan(step, init, None, length=L)
            return (i_idx, j_idx, valid)

        def _align_one(small, large):
            T_small, d = small.shape
            T_large = large.shape[0]
            D = _pairwise_euclidean(small, large)
            R = _dtw_cost(D)
            i_idx, j_idx, valid = _backtrack(R, T_small, T_large)
            contrib = small[i_idx] * valid[:, None].astype(small.dtype)
            expanded = jnp.zeros((T_large, d), dtype=small.dtype).at[j_idx].add(contrib)
            return expanded
        return jax.vmap(_align_one)(teacher_features, student_features)

    def _L0_ffn_ref(x, gate_w, gate_b, w1, b1, w2, b2):
        import jax, jax.numpy as jnp
        import numpy as np
        B, S, D, E, K = (4, 256, 128, 8, 2)
        H = 4 * D
        Bx, Sx, Dx = x.shape
        n_exp = w1.shape[0]
        logits = jnp.einsum('bsd,de->bse', x, gate_w) + gate_b
        scores = jax.nn.softmax(logits, axis=-1)
        topk_s, topk_i = jax.lax.top_k(scores, K)
        onehot = jax.nn.one_hot(topk_i, n_exp, dtype=scores.dtype)
        dispatch = jnp.einsum('bske,bsk->bse', onehot, topk_s)
        xf = x.reshape(-1, Dx)
        wf = dispatch.reshape(-1, n_exp)
        out = jnp.zeros_like(xf)
        for i in range(n_exp):
            wi = wf[:, i:i + 1]
            h = jax.nn.relu(xf * wi @ w1[i] + b1[i])
            y = h @ w2[i] + b2[i]
            out = jnp.where(wi > 0, y, out)
        return out.reshape(Bx, Sx, Dx)
    x = x + _L0_attn_ref(_layernorm(x, axis=-1), L0_attn_qkv_w, L0_attn_qkv_b, L0_attn_out_w, L0_attn_out_b)
    x = x + _L0_xattn_ref(ctx_1024, _layernorm(x, axis=-1))
    x = x + _L0_ffn_ref(_layernorm(x, axis=-1), L0_ffn_gate_w, L0_ffn_gate_b, L0_ffn_w1, L0_ffn_b1, L0_ffn_w2, L0_ffn_b2)
    return x

_drawn_inputs = setup_inputs


def setup_inputs(seed=0):
    import zlib

    import numpy as np

    out = dict(_drawn_inputs(seed))
    spreads = {'L0_attn_qkv_b': (0.0, 0.1),
     'L0_attn_out_b': (0.0, 0.1),
     'L0_ffn_gate_b': (0.0, 0.1),
     'L0_ffn_b1': (0.0, 0.1),
     'L0_ffn_b2': (0.0, 0.1)}
    factors = {}
    for name, (base, spread) in spreads.items():
        noise = np.random.default_rng([zlib.crc32(name.encode()), seed]).standard_normal(out[name].shape)
        drawn = base * np.exp(spread * noise) if base else spread * noise
        out[name] = jnp.asarray(drawn.astype(out[name].dtype))
    for name, factor in factors.items():
        out[name] = (out[name] * factor).astype(out[name].dtype)
    return out
```

```python
from contextlib import ExitStack

import concourse.bass as bass
from concourse import mybir

F32 = mybir.dt.float32
I32 = mybir.dt.int32
ALU = mybir.AluOpType
ACT = mybir.ActivationFunctionType
AX_X = mybir.AxisListType.X

P = 128
T, J = 2, 512
NT = T * J // P
TPB = J // P
HEADS, DH = 16, 8
MASKED = -10000.0
EPS = 1e-5
ROWS = 77
BIG = 1e30
CH, CW = 16, J // 16
STEPS = ROWS + CH - 1
LANES = 64
NE, HID = 8, 512
HC = HID // P
HID_BANKS = [0, 1, 4, 5]
Y_BANKS = [2, 3, 6, 7]


def build(nc, x, ctx_rows, ctx_t, qkv_wt, qkv_b, out_wt, out_b, gate_w, gate_b, w1, b1, w2, b2, out):
    with ExitStack() as stack:
        def sb(name, shape, dt=F32):
            return stack.enter_context(nc.sbuf_tensor(name, shape, dt))

        attention_only = ExitStack()

        def early(name, shape, dt=F32):
            return attention_only.enter_context(nc.sbuf_tensor(name, shape, dt))

        def sem(name):
            return stack.enter_context(nc.semaphore(name))

        ident = sb("ident", [P, P])
        ones = sb("ones", [P, P])
        eps_col = sb("eps_col", [P, 1])
        X = sb("X", [P, NT, P])
        stats = sb("stats", [P, 3, NT, 6])
        mean_var = sb("mean_var", [P, 3, NT, 2])
        std = sb("std", [P, 3, NT])
        rstd = sb("rstd", [P, 3, NT])
        X1 = sb("X1", [P, NT, P])
        S = sb("S", [P, NT, P])
        ST = sb("ST", [P, NT * P])
        SQ = sb("SQ", [P, NT * P])
        ctxT = sb("ctxT", [P, T * ROWS])
        ctxTm2 = sb("ctxTm2", [P, T * ROWS])
        ctxr = sb("ctxr", [ROWS, T, P])
        ctxsq = sb("ctxsq", [ROWS, T, P])
        aa = sb("aa", [ROWS, T])
        D = sb("D", [ROWS, T, J])
        Dsk = sb("Dsk", [LANES, STEPS, CW + 1])
        M = sb("M", [LANES, STEPS, CW + 1])
        R = sb("R", [LANES, STEPS + 1, CW + 1])
        dg = sb("dg", [LANES, STEPS, CW], mybir.dt.bfloat16)
        notleft = sb("notleft", [LANES, STEPS, CW], mybir.dt.bfloat16)
        V = sb("V", [LANES, STEPS, CW])
        col2 = sb("col2", [LANES, CW])
        Vr = sb("Vr", [ROWS, T, J])
        table = sb("table", [ROWS, T, 2, J], I32)
        iota_f = sb("iota_f", [ROWS, J])
        picked = sb("picked", [ROWS, T, 2, ROWS])
        diag = sb("diag", [ROWS, T, 2, ROWS])
        rowsc = sb("rowsc", [ROWS, T, 2])
        upto = sb("upto", [ROWS, T, J])
        onpath = sb("onpath", [ROWS, T, J])
        gw = sb("gw", [P, NE])
        gb = sb("gb", [P, NE])
        logit = sb("logit", [P, NT, NE])
        lmax = sb("lmax", [P, NT])
        lsh = sb("lsh", [P, NT, NE])
        lexp = sb("lexp", [P, NT, NE])
        lsum = sb("lsum", [P, NT])
        lrec = sb("lrec", [P, NT])
        gs = sb("gs", [P, NT, NE])
        lower = sb("lower", [P, NE, NE])
        upper = sb("upper", [P, NE, NE])
        rank = sb("rank", [P, NT, NE])
        top2 = sb("top2", [P, NT, NE])
        key = sb("key", [P, NT, NE])
        e1 = sb("e1", [P, NE])
        last = sb("last", [P, NT])
        onehot = sb("onehot", [P, NT, NE])
        wsel = sb("wsel", [P, NT, NE])
        wgate = sb("wgate", [P, NT])
        onehotT = sb("onehotT", [NE, NT * P])
        W1 = sb("W1", [P, NE, HID])
        W2 = sb("W2", [P, NE, HC, P])
        B1 = sb("B1", [P, NE, HC])
        B2 = sb("B2", [NE, P])
        XB = early("XB", [P, NT, P])
        H = early("H", [P, NT, P])
        HT = early("HT", [P, NT * P])
        wqkv = early("wqkv", [P, 3 * P])
        bqkv = early("bqkv", [P, 3 * P])
        wo = early("wo", [P, P])
        bo = early("bo", [P, P])
        QKV = early("QKV", [P, NT, 3 * P])
        dk = early("dk", [P, TPB, P])
        dv = early("dv", [P, TPB, P])
        prod = early("prod", [P, T, TPB, P])
        score = early("score", [P, T, TPB * HEADS])
        dif = early("dif", [P, T, TPB * HEADS])
        dif_hi = early("dif_hi", [P, T, TPB * HEADS])
        dif_lo = early("dif_lo", [P, T, TPB * HEADS])
        exp_old = early("exp_old", [P, T, TPB * HEADS])
        exp_new = early("exp_new", [P, T, TPB * HEADS])
        exp_sum = early("exp_sum", [P, T, TPB * HEADS])
        exp_rec = early("exp_rec", [P, T, TPB * HEADS])
        prob = early("prob", [P, T, TPB * HEADS])
        pdv = early("pdv", [P, T, TPB, P])
        att = early("att", [P, NT, P])
        attT = early("attT", [P, NT * P])
        attention_only.close()
        X2 = sb("X2", [P, NT, P])
        F = sb("F", [P, NT, P])
        FT = sb("FT", [P, NT * P])
        FS = sb("FS", [P, NT, P])
        FST = sb("FST", [P, NT * P])
        ge = sb("ge", [P, NT, NE, NE])
        gt = sb("gt", [P, NT, NE, NE])
        ahead = sb("ahead", [P, NT, NE, NE])
        HH = sb("HH", [P, 2, HC, J])
        ACC = sb("ACC", [P, NT, P])
        banks = [stack.enter_context(nc.psum_tensor(f"bank{i}", [P, 512], F32)) for i in range(8)]
        d_scratch = nc.dram_tensor("d_scratch", (T, CH, STEPS, CW + 1), F32)
        v_scratch = nc.dram_tensor("v_scratch", (T, CH, STEPS, CW), F32)

        x_in = sem("x_in"); attn_in = sem("attn_in"); ctx_in = sem("ctx_in")
        moe_in = sem("moe_in"); out_done = sem("out_done")
        const_done = sem("const_done"); pool_step = sem("pool_step"); lanes_done = sem("lanes_done")
        dve_step = sem("dve_step"); act_step = sem("act_step")
        var_done = sem("var_done"); std_done = sem("std_done"); norm_done = sem("norm_done")
        tr_done = sem("tr_done"); tr_copied = sem("tr_copied")
        qkv_done = sem("qkv_done"); qkv_copied = sem("qkv_copied")
        xb_done = sem("xb_done"); split_done = sem("split_done"); exp_done = sem("exp_done")
        att_done = sem("att_done"); proj_done = sem("proj_done"); x1_done = sem("x1_done")
        m2_done = sem("m2_done"); sq_done = sem("sq_done"); dist_done = sem("dist_done")
        d2_done = sem("d2_done"); d_done = sem("d_done")
        prefill = sem("prefill"); d_out = sem("d_out"); dsk_in = sem("dsk_in")
        low_done = sem("low_done"); scan_done = sem("scan_done"); mask_done = sem("mask_done")
        v_done = sem("v_done"); v_out = sem("v_out"); v_in = sem("v_in")
        table_done = sem("table_done"); picked0 = sem("picked0"); picked1 = sem("picked1")
        path_done = sem("path_done"); exp2_done = sem("exp2_done"); x2_done = sem("x2_done")
        logit_done = sem("logit_done"); lsh_done = sem("lsh_done"); lexp_done = sem("lexp_done")
        hot_done = sem("hot_done"); fs_done = sem("fs_done")
        hid_done = sem("hid_done"); hid_copied = sem("hid_copied")
        y_done = sem("y_done"); acc_done = sem("acc_done"); bias_done = sem("bias_done")

        block = stack.enter_context(nc.Block())
        x_v = x.rearrange("t (n p) d -> p (t n) d", p=P)
        out_v = out.rearrange("t (n p) d -> p (t n) d", p=P)
        SK = CW + 1

        @block.sync
        def _(sp):
            sp.dma_start(X[:], x_v).then_inc(x_in, 16)
            sp.dma_start(wqkv[:], qkv_wt).then_inc(attn_in, 16)
            sp.dma_start(bqkv[:], qkv_b.partition_broadcast(P)).then_inc(attn_in, 16)
            sp.dma_start(wo[:], out_wt).then_inc(attn_in, 16)
            sp.dma_start(bo[:], out_b.partition_broadcast(P)).then_inc(attn_in, 16)
            sp.dma_start(ctxT[:], ctx_t).then_inc(ctx_in, 16)
            sp.dma_start(ctxr[:], ctx_rows.rearrange("t r d -> r t d")).then_inc(ctx_in, 16)
            sp.dma_start(gw[:], gate_w).then_inc(moe_in, 16)
            sp.dma_start(gb[:], gate_b.partition_broadcast(P)).then_inc(moe_in, 16)
            sp.dma_start(B1[:], b1).then_inc(moe_in, 16)
            sp.dma_start(B2[:], b2).then_inc(moe_in, 16)
            sp.wait_ge(lanes_done, 1)
            for b in range(T):
                sp.dma_start(d_scratch.ap()[b], Dsk[32 * b:32 * b + CH]).then_inc(prefill, 16)
            sp.dma_start(W1[:], w1.rearrange("e d h -> d e h")).then_inc(moe_in, 16)
            sp.dma_start(W2[:], w2.rearrange("e (c p) d -> p e c d", p=P)).then_inc(moe_in, 16)
            sp.wait_ge(prefill, 32)
            for b in range(T):
                sp.wait_ge(d_done, b + 1)
                dst = bass.AP(d_scratch, b * CH * STEPS * SK + 1, [[SK, ROWS], [STEPS * SK + SK, CH], [1, CW]])
                sp.dma_start(dst, D[:, b, :].rearrange("r (c w) -> r c w", w=CW)).then_inc(d_out, 16)
            sp.wait_ge(d_out, 32)
            for b in range(T):
                sp.dma_start(Dsk[32 * b:32 * b + CH], d_scratch.ap()[b]).then_inc(dsk_in, 16)
            for b in range(T):
                sp.wait_ge(v_done, 1)
                sp.dma_start(v_scratch.ap()[b], V[32 * b:32 * b + CH]).then_inc(v_out, 16)
            sp.wait_ge(v_out, 32)
            for b in range(T):
                src = bass.AP(v_scratch, b * CH * STEPS * CW, [[CW, ROWS], [STEPS * CW + CW, CH], [1, CW]])
                sp.dma_start(Vr[:, b, :].rearrange("r (c w) -> r c w", w=CW), src).then_inc(v_in, 16)
            sp.wait_ge(acc_done, T * (NE + 1))
            sp.dma_start(out_v, ACC[:]).then_inc(out_done, 16)
            sp.wait_ge(out_done, 16)

        @block.gpsimd
        def _(pool):
            steps = [0]

            def step(i):
                steps[0] += 1
                i.then_inc(pool_step, 1)
                pool.wait_ge(pool_step, steps[0])

            def lanes(b):
                return slice(32 * b, 32 * b + 32)

            step(nc.gpsimd.memset(ident[:], 0.0))
            step(nc.gpsimd.affine_select(out=ident[:], in_=ident[:], pattern=[[-1, P]], compare_op=ALU.not_equal,
                                         fill=1.0, base=0, channel_multiplier=1))
            step(nc.gpsimd.memset(ones[:], 1.0))
            step(nc.gpsimd.memset(eps_col[:], EPS))
            pool.sem_inc(const_done, 1)
            step(nc.gpsimd.memset(Dsk[:], BIG))
            step(nc.gpsimd.memset(Dsk[:, :, 0:1], 0.0))
            step(nc.gpsimd.memset(R[:, 0, :], BIG))
            for b in range(T):
                step(nc.gpsimd.memset(R[32 * b:32 * b + 1, 0, 0:1], 0.0))
            pool.sem_inc(lanes_done, 1)
            for b in range(T):
                step(nc.gpsimd.iota(col2[lanes(b), :], pattern=[[2, CW]], base=0, channel_multiplier=2 * CW,
                                    allow_small_or_imprecise_dtypes=True))
            step(nc.gpsimd.iota(iota_f[:], pattern=[[1, J]], base=0, channel_multiplier=0,
                                allow_small_or_imprecise_dtypes=True))
            for b in range(T):
                step(nc.gpsimd.iota(table[:, b, 1, :], pattern=[[1, J]], base=0, channel_multiplier=0))
            step(nc.gpsimd.iota(e1[:], pattern=[[1, NE]], base=1, channel_multiplier=0,
                                allow_small_or_imprecise_dtypes=True))
            step(nc.gpsimd.memset(lower[:], 1.0))
            step(nc.gpsimd.affine_select(out=lower[:], in_=lower[:], pattern=[[1, NE], [-1, NE]],
                                         compare_op=ALU.is_gt, fill=0.0, base=0, channel_multiplier=0))
            step(nc.gpsimd.memset(upper[:], 1.0))
            step(nc.gpsimd.affine_select(out=upper[:], in_=upper[:], pattern=[[-1, NE], [1, NE]],
                                         compare_op=ALU.is_ge, fill=0.0, base=0, channel_multiplier=0))
            pool.sem_inc(const_done, 1)
            pool.wait_ge(x_in, 16)
            pool.wait_ge(attn_in, 64)
            step(nc.gpsimd.tensor_tensor(XB[:], X[:], bo[:].unsqueeze(1).to_broadcast([P, NT, P]), ALU.add))
            pool.sem_inc(xb_done, 1)
            pool.wait_ge(mask_done, 2 * STEPS)
            step(nc.gpsimd.tensor_tensor(V[:], col2[:].unsqueeze(1).to_broadcast([LANES, STEPS, CW]), dg[:],
                                         ALU.subtract))
            nc.gpsimd.tensor_tensor(V[:], V[:], notleft[:], ALU.mult).then_inc(v_done, 1)

        def follow_path(eng, copy, b, done):
            eng.wait_ge(table_done, b + 1)
            eng.wait_ge(const_done, 2)
            col = J - 1
            for i in range(ROWS - 1, -1, -1):
                copy(picked[:, b, :, i], table[:, b, :, bass.ds(col, 1)].squeeze(2)).then_inc(done, 1)
                if i:
                    code = eng.value_load(table[i:i + 1, b, 0, bass.ds(col, 1)])
                    col = nc.s_assert_within(code // 2, 0, J - 1, skip_runtime_bounds_check_because=
                                             "a code is twice a column of the row, or one less")

        @block.vector
        def _(dve):
            steps = [0]

            def step(i):
                steps[0] += 1
                i.then_inc(dve_step, 1)
                dve.wait_ge(dve_step, steps[0])

            def norm(k, src, dst, ready, need):
                dve.wait_ge(ready, need)
                for n in range(NT):
                    i = nc.vector.bn_stats(stats[:, k, n, :], src[:, n, :])
                step(i)
                for n in range(NT):
                    i = nc.vector.bn_aggr(mean_var[:, k, n, :], stats[:, k, n, :])
                i.then_inc(var_done, 1)
                dve.wait_ge(std_done, k + 1)
                step(nc.vector.reciprocal(rstd[:, k, :], std[:, k, :]))
                for n in range(NT):
                    i = nc.vector.tensor_scalar(dst[:, n, :], src[:, n, :], mean_var[:, k, n, 0:1],
                                                rstd[:, k, n:n + 1], ALU.subtract, ALU.mult)
                i.then_inc(norm_done, 1)

            norm(0, X, H, x_in, 16)
            dve.wait_ge(attn_in, 64)
            for n in range(NT):
                dve.wait_ge(qkv_done, n + 1)
                nc.vector.tensor_tensor(QKV[:, n, :], banks[(n + 2) % 8][:, 0:3 * P], bqkv[:],
                                        ALU.add).then_inc(qkv_copied, 1)
            dve.wait_ge(qkv_copied, NT)
            q, k, v = (QKV[:, :, i * P:(i + 1) * P] for i in range(3))
            t0, t1 = slice(0, TPB), slice(TPB, NT)
            nc.vector.tensor_tensor(prod[:, 0], q[:, t0, :], k[:, t0, :], ALU.mult)
            step(nc.vector.tensor_tensor(dk[:], k[:, t1, :], k[:, t0, :], ALU.subtract))
            nc.vector.tensor_tensor(dv[:], v[:, t1, :], v[:, t0, :], ALU.subtract)
            step(nc.vector.tensor_tensor(prod[:, 1], q[:, t1, :], dk[:], ALU.mult))
            step(nc.vector.tensor_reduce(score[:], prod[:].rearrange("p t n (h d) -> p t (n h) d", d=DH),
                                         AX_X, ALU.add))
            nc.vector.tensor_scalar(dif[:, 0], score[:, 0], -(DH ** -0.5), MASKED, ALU.mult, ALU.add)
            step(nc.vector.tensor_scalar(dif[:, 1], score[:, 1], DH ** -0.5, None, ALU.mult))
            nc.vector.tensor_scalar(dif_hi[:], dif[:], 0.0, None, ALU.max)
            nc.vector.tensor_scalar(dif_lo[:], dif[:], 0.0, None, ALU.min).then_inc(split_done, 1)
            dve.wait_ge(exp_done, 2)
            step(nc.vector.tensor_tensor(exp_sum[:], exp_old[:], exp_new[:], ALU.add))
            step(nc.vector.reciprocal(exp_rec[:], exp_sum[:]))
            step(nc.vector.tensor_tensor(prob[:], exp_new[:], exp_rec[:], ALU.mult))
            for t in range(T):
                i = nc.vector.tensor_tensor(
                    pdv[:, t].rearrange("p n (h d) -> p (n h) d", d=DH),
                    prob[:, t].unsqueeze(2).to_broadcast([P, TPB * HEADS, DH]),
                    dv[:].rearrange("p n (h d) -> p (n h) d", d=DH), ALU.mult)
            step(i)
            for t in range(T):
                i = nc.vector.tensor_tensor(att[:, t * TPB:(t + 1) * TPB, :], pdv[:, t], v[:, t0, :], ALU.add)
            i.then_inc(att_done, 1)
            dve.wait_ge(xb_done, 1)
            for t in range(T):
                dve.wait_ge(proj_done, t + 1)
                nc.vector.tensor_tensor(X1[:, t * TPB:(t + 1) * TPB, :],
                                        banks[4 + t][:].rearrange("p (n d) -> p n d", d=P),
                                        XB[:, t * TPB:(t + 1) * TPB, :], ALU.add).then_inc(x1_done, 1)
            norm(1, X1, S, x1_done, 2)
            dve.wait_ge(ctx_in, 32)
            nc.vector.tensor_scalar(ctxTm2[:], ctxT[:], -2.0, None, ALU.mult).then_inc(m2_done, 1)
            step(nc.vector.tensor_tensor(ctxsq[:], ctxr[:], ctxr[:], ALU.mult))
            step(nc.vector.tensor_reduce(aa[:], ctxsq[:], AX_X, ALU.add))
            for b in range(T):
                dve.wait_ge(dist_done, b + 1)
                nc.vector.tensor_scalar(D[:, b, :], banks[b][0:ROWS, :], aa[:, b:b + 1], 0.0, ALU.add,
                                        ALU.max).then_inc(d2_done, 1)

            shift = [CH] + list(range(CH - 1)) + [CH] + list(range(CH, 31))
            dve.wait_ge(lanes_done, 1)
            dve.wait_ge(dsk_in, 32)
            for s in range(STEPS):
                if s:
                    dve.wait_ge(scan_done, s)
                nc.vector.tensor_tensor(M[:, s, 1:SK], R[:, s, 1:SK], R[:, s, 0:CW], ALU.min).then_inc(low_done, 1)
                nc.vector.stream_shuffle(M[:, s, 0:1], R[:, s, CW:SK], shift).then_inc(low_done, 1)
                nc.vector.tensor_tensor(dg[:, s, :], R[:, s, 0:CW], R[:, s, 1:SK], ALU.is_le).then_inc(mask_done, 1)
                dve.wait_ge(low_done, 2 * s + 2)
                nc.vector.tensor_tensor_scan(R[:, s + 1, :], M[:, s, :], Dsk[:, s, :], BIG, ALU.min,
                                             ALU.add).then_inc(scan_done, 1)
                if s:
                    nc.vector.tensor_tensor(notleft[:, s - 1, :], R[:, s, 0:CW], M[:, s - 1, 1:SK],
                                            ALU.is_ge).then_inc(mask_done, 1)
            dve.wait_ge(scan_done, STEPS)
            nc.vector.tensor_tensor(notleft[:, STEPS - 1, :], R[:, STEPS, 0:CW], M[:, STEPS - 1, 1:SK],
                                    ALU.is_ge).then_inc(mask_done, 1)
            dve.wait_ge(v_in, 32)
            for b in range(T):
                nc.vector.tensor_tensor_scan(table[:, b, 0, :], Vr[:, b, :], Vr[:, b, :], 0.0, ALU.max,
                                             ALU.max).then_inc(table_done, 1)
            follow_path(dve, nc.vector.tensor_copy, 1, picked1)

            dve.wait_ge(picked0, ROWS)
            dve.wait_ge(picked1, ROWS)
            step(nc.vector.tensor_tensor(diag[:].rearrange("r b q i -> r (b q) i"),
                                         picked[:].rearrange("r b q i -> r (b q) i"),
                                         ident[0:ROWS, 0:ROWS].unsqueeze(1).to_broadcast([ROWS, 2 * T, ROWS]), ALU.mult))
            step(nc.vector.tensor_reduce(rowsc[:], diag[:], AX_X, ALU.add))
            for b in range(T):
                i = nc.vector.tensor_scalar(upto[:, b, :], iota_f[:], rowsc[:, b, 1:2], None, ALU.is_le)
            step(i)
            for b in range(T):
                nc.vector.scalar_tensor_tensor(out=onpath[:, b, :], in0=table[:, b, 0, :], scalar=rowsc[:, b, 0:1],
                                               in1=upto[:, b, :], op0=ALU.is_equal,
                                               op1=ALU.mult).then_inc(path_done, 1)
            for b in range(T):
                dve.wait_ge(exp2_done, b + 1)
                nc.vector.tensor_tensor(X2[:, b * TPB:(b + 1) * TPB, :],
                                        banks[2 + b][:].rearrange("p (n d) -> p n d", d=P),
                                        X1[:, b * TPB:(b + 1) * TPB, :], ALU.add).then_inc(x2_done, 1)
            norm(2, X2, F, x2_done, 2)

            dve.wait_ge(const_done, 2)
            dve.wait_ge(moe_in, 96)
            dve.wait_ge(logit_done, 1)
            step(nc.vector.tensor_tensor(logit[:], banks[6][:, 0:NT * NE].rearrange("p (n e) -> p n e", e=NE),
                                         gb[:].unsqueeze(1).to_broadcast([P, NT, NE]), ALU.add))
            step(nc.vector.tensor_reduce(lmax[:], logit[:], AX_X, ALU.max))
            nc.vector.tensor_tensor(lsh[:], logit[:], lmax[:].unsqueeze(2).to_broadcast([P, NT, NE]),
                                    ALU.subtract).then_inc(lsh_done, 1)
            dve.wait_ge(lexp_done, 1)
            step(nc.vector.tensor_reduce(lsum[:], lexp[:], AX_X, ALU.add))
            step(nc.vector.reciprocal(lrec[:], lsum[:]))
            step(nc.vector.tensor_tensor(gs[:], lexp[:], lrec[:].unsqueeze(2).to_broadcast([P, NT, NE]), ALU.mult))
            mine = gs[:].unsqueeze(3).to_broadcast([P, NT, NE, NE])
            theirs = gs[:].unsqueeze(2).to_broadcast([P, NT, NE, NE])
            nc.vector.tensor_tensor(ge[:], theirs, mine, ALU.is_ge)
            step(nc.vector.tensor_tensor(gt[:], theirs, mine, ALU.is_gt))
            flat = "p n e f -> p n (e f)"
            lo_b = lower[:].rearrange("p e f -> p (e f)").unsqueeze(1).to_broadcast([P, NT, NE * NE])
            up_b = upper[:].rearrange("p e f -> p (e f)").unsqueeze(1).to_broadcast([P, NT, NE * NE])
            nc.vector.tensor_tensor(ge[:].rearrange(flat), ge[:].rearrange(flat), lo_b, ALU.mult)
            step(nc.vector.tensor_tensor(gt[:].rearrange(flat), gt[:].rearrange(flat), up_b, ALU.mult))
            step(nc.vector.tensor_tensor(ahead[:], ge[:], gt[:], ALU.add))
            step(nc.vector.tensor_reduce(rank[:], ahead[:], AX_X, ALU.add))
            step(nc.vector.tensor_scalar(top2[:], rank[:], 1.5, None, ALU.is_lt))
            step(nc.vector.scalar_tensor_tensor(out=top2[:], in0=gs[:], scalar=0.0, in1=top2[:], op0=ALU.is_gt,
                                                op1=ALU.mult))
            step(nc.vector.tensor_tensor(key[:], top2[:], e1[:].unsqueeze(1).to_broadcast([P, NT, NE]), ALU.mult))
            step(nc.vector.tensor_reduce(last[:], key[:], AX_X, ALU.max))
            step(nc.vector.tensor_tensor(onehot[:], key[:], last[:].unsqueeze(2).to_broadcast([P, NT, NE]),
                                         ALU.is_equal))
            step(nc.vector.tensor_tensor(onehot[:], onehot[:], top2[:], ALU.mult))
            step(nc.vector.tensor_tensor(wsel[:], onehot[:], gs[:], ALU.mult))
            nc.vector.tensor_reduce(wgate[:], wsel[:], AX_X, ALU.add).then_inc(hot_done, 1)
            dve.wait_ge(hot_done, 1)
            for n in range(NT):
                i = nc.vector.tensor_scalar(FS[:, n, :], F[:, n, :], wgate[:, n:n + 1], None, ALU.mult)
            i.then_inc(fs_done, 1)
            for t in range(T):
                dve.wait_ge(bias_done, t + 1)
                nc.vector.tensor_tensor(ACC[:, t * TPB:(t + 1) * TPB, :], X2[:, t * TPB:(t + 1) * TPB, :],
                                        banks[Y_BANKS[2 + t]][:].rearrange("p (n d) -> p n d", d=P),
                                        ALU.add).then_inc(acc_done, 1)
            for e in range(NE):
                for t in range(T):
                    k = e * T + t
                    dve.wait_ge(y_done, k + 1)
                    dve.wait_ge(acc_done, k + 1)
                    for n in range(TPB):
                        i = nc.vector.scalar_tensor_tensor(
                            out=ACC[:, t * TPB + n, :], in0=banks[Y_BANKS[k % 4]][:, n * P:(n + 1) * P],
                            scalar=onehot[:, t * TPB + n, e:e + 1], in1=ACC[:, t * TPB + n, :],
                            op0=ALU.mult, op1=ALU.add)
                    i.then_inc(acc_done, 1)

        @block.scalar
        def _(act):
            act.wait_ge(const_done, 1)

            def root(k):
                act.wait_ge(var_done, k + 1)
                nc.scalar.activation(std[:, k, :], mean_var[:, k, :, 1], ACT.Sqrt, bias=eps_col[:]).then_inc(std_done, 1)

            def copy_t(dst, first_bank, count):
                for t in range(T):
                    act.wait_ge(tr_done, count + t + 1)
                    nc.scalar.copy(dst[:, t * J:(t + 1) * J], banks[first_bank + t][:]).then_inc(tr_copied, 1)

            root(0)
            copy_t(HT, 0, 0)
            act.wait_ge(split_done, 1)
            nc.scalar.activation(exp_old[:], dif_hi[:], ACT.Exp, scale=-1.0).then_inc(exp_done, 1)
            nc.scalar.activation(exp_new[:], dif_lo[:], ACT.Exp).then_inc(exp_done, 1)
            copy_t(attT, 2, 2)
            root(1)
            for t in range(T):
                act.wait_ge(tr_done, 4 + t + 1)
                nc.scalar.copy(ST[:, t * J:(t + 1) * J], banks[6 + t][:]).then_inc(tr_copied, 1)
                nc.scalar.activation(SQ[:, t * J:(t + 1) * J], banks[6 + t][:], ACT.Square).then_inc(sq_done, 1)
            for b in range(T):
                act.wait_ge(d2_done, b + 1)
                nc.scalar.activation(D[:, b, :], D[:, b, :], ACT.Sqrt).then_inc(d_done, 1)
            follow_path(act, nc.scalar.copy, 0, picked0)
            root(2)
            copy_t(FT, 4, 6)
            act.wait_ge(lsh_done, 1)
            nc.scalar.activation(lexp[:], lsh[:], ACT.Exp).then_inc(lexp_done, 1)
            copy_t(FST, 4, 8)
            act.wait_ge(tr_done, 12)
            for t in range(T):
                nc.scalar.copy(onehotT[:, t * J:(t + 1) * J], banks[t][0:NE, :]).then_inc(tr_copied, 1)
            act.wait_ge(moe_in, 96)
            for e in range(NE):
                for t in range(T):
                    k = e * T + t
                    for c in range(HC):
                        act.wait_ge(hid_done, k * HC + c + 1)
                        if k >= 2 and c == 0:
                            act.wait_ge(y_done, k - 1)
                        nc.scalar.activation(HH[:, k % 2, c, :], banks[HID_BANKS[c]][:], ACT.Relu,
                                             bias=B1[:, e, c:c + 1]).then_inc(hid_copied, 1)

        @block.tensor
        def _(pe):
            pe.wait_ge(const_done, 1)

            def transposes(src, first_bank, only_half=None):
                for n in range(NT):
                    i = nc.tensor.transpose(banks[first_bank + n // TPB][:, (n % TPB) * P:(n % TPB + 1) * P],
                                            src[:, n, :], ident[:])
                    if n % TPB == TPB - 1:
                        i.then_inc(tr_done, 1)

            pe.wait_ge(norm_done, 1)
            transposes(H, 0)
            pe.wait_ge(attn_in, 64)
            pe.wait_ge(tr_copied, 2)
            for n in range(NT):
                nc.tensor.matmul(banks[(n + 2) % 8][:, 0:3 * P], HT[:, n * P:(n + 1) * P], wqkv[:],
                                 start=True, stop=True).then_inc(qkv_done, 1)
            pe.wait_ge(att_done, 1)
            transposes(att, 2)
            pe.wait_ge(tr_copied, 4)
            for n in range(NT):
                i = nc.tensor.matmul(banks[4 + n // TPB][:, (n % TPB) * P:(n % TPB + 1) * P],
                                     attT[:, n * P:(n + 1) * P], wo[:], start=True, stop=True)
                if n % TPB == TPB - 1:
                    i.then_inc(proj_done, 1)
            pe.wait_ge(norm_done, 2)
            transposes(S, 6)
            pe.wait_ge(m2_done, 1)
            for b in range(T):
                pe.wait_ge(sq_done, b + 1)
                nc.tensor.matmul(banks[b][0:ROWS, :], ones[:, 0:ROWS], SQ[:, b * J:(b + 1) * J], start=True, stop=False)
                nc.tensor.matmul(banks[b][0:ROWS, :], ctxTm2[:, b * ROWS:(b + 1) * ROWS], ST[:, b * J:(b + 1) * J],
                                 start=False, stop=True).then_inc(dist_done, 1)
            for b in range(T):
                pe.wait_ge(path_done, b + 1)
                for n in range(TPB):
                    i = nc.tensor.matmul(banks[2 + b][:, n * P:(n + 1) * P], onpath[:, b, n * P:(n + 1) * P],
                                         ctxr[:, b, :], start=True, stop=True)
                i.then_inc(exp2_done, 1)
            pe.wait_ge(norm_done, 3)
            transposes(F, 4)
            pe.wait_ge(tr_copied, 8)
            pe.wait_ge(moe_in, 96)
            for n in range(NT):
                i = nc.tensor.matmul(banks[6][:, n * NE:(n + 1) * NE], FT[:, n * P:(n + 1) * P], gw[:],
                                     start=True, stop=True)
            i.then_inc(logit_done, 1)
            pe.wait_ge(fs_done, 1)
            transposes(FS, 4)
            pe.wait_ge(hot_done, 1)
            for n in range(NT):
                i = nc.tensor.transpose(banks[n // TPB][0:NE, (n % TPB) * P:(n % TPB + 1) * P], onehot[:, n, :],
                                        ident[:])
                if n % TPB == TPB - 1:
                    i.then_inc(tr_done, 1)
            pe.wait_ge(tr_copied, 12)
            for t in range(T):
                for n in range(TPB):
                    i = nc.tensor.matmul(banks[Y_BANKS[2 + t]][:, n * P:(n + 1) * P],
                                         onehotT[:, t * J + n * P:t * J + (n + 1) * P], B2[:], start=True, stop=True)
                i.then_inc(bias_done, 1)
            for e in range(NE):
                for t in range(T):
                    k = e * T + t
                    for c in range(HC):
                        if k:
                            pe.wait_ge(hid_copied, (k - 1) * HC + c + 1)
                        nc.tensor.matmul(banks[HID_BANKS[c]][:], W1[:, e, c * P:(c + 1) * P],
                                         FST[:, t * J:(t + 1) * J], start=True, stop=True).then_inc(hid_done, 1)
                    pe.wait_ge(hid_copied, (k + 1) * HC)
                    if k >= 2:
                        pe.wait_ge(acc_done, k)
                    for n in range(TPB):
                        for c in range(HC):
                            i = nc.tensor.matmul(banks[Y_BANKS[k % 4]][:, n * P:(n + 1) * P],
                                                 HH[:, k % 2, c, n * P:(n + 1) * P], W2[:, e, c, :],
                                                 start=(c == 0), stop=(c == HC - 1))
                    i.then_inc(y_done, 1)


def kernel(x, ctx_1024, L0_attn_qkv_w, L0_attn_qkv_b, L0_attn_out_w, L0_attn_out_b, L0_ffn_gate_w,
           L0_ffn_gate_b, L0_ffn_w1, L0_ffn_b1, L0_ffn_w2, L0_ffn_b2):
    import numpy as np
    import concourse.bacc as bacc
    from concourse import mybir
    from concourse.bass_utils import run_bass_kernel_spmd

    nc = bacc.Bacc("TRN2", target_bir_lowering=False, num_devices=1)
    given = {
        "x": x, "ctx_rows": ctx_1024,
        "ctx_t": np.transpose(np.asarray(ctx_1024), (2, 0, 1)).reshape(128, -1),
        "qkv_wt": np.transpose(np.asarray(L0_attn_qkv_w)), "qkv_b": L0_attn_qkv_b,
        "out_wt": np.transpose(np.asarray(L0_attn_out_w)), "out_b": L0_attn_out_b,
        "gate_w": L0_ffn_gate_w, "gate_b": L0_ffn_gate_b,
        "w1": L0_ffn_w1, "b1": np.transpose(np.asarray(L0_ffn_b1).reshape(8, 4, 128), (2, 0, 1)), "w2": L0_ffn_w2, "b2": L0_ffn_b2,
    }
    arrays, aps = {}, {}
    for name, a in given.items():
        a = np.ascontiguousarray(a)
        arrays["in_" + name] = a
        aps[name] = nc.dram_tensor("in_" + name, a.shape, mybir.dt.from_np(a.dtype), kind="ExternalInput").ap()
    out = nc.dram_tensor("out_0", (2, 512, 128), mybir.dt.float32, kind="ExternalOutput").ap()
    build(nc, out=out, **aps)
    r = run_bass_kernel_spmd(nc, [arrays], core_ids=[0])
    return r.results[0]["out_0"]
```

```python
from contextlib import ExitStack

import concourse.bass as bass
from concourse import mybir

F32 = mybir.dt.float32
I32 = mybir.dt.int32
U32 = mybir.dt.uint32
BF16 = mybir.dt.bfloat16
ALU = mybir.AluOpType
ACT = mybir.ActivationFunctionType
AX_X = mybir.AxisListType.X

P = 128
T, J = 2, 512
NT = T * J // P
TPB = J // P
HEADS, DH = 16, 8
MASKED = -10000.0
EPS = 1e-5
ROWS = 77
BIG = 1e30
CH, CW = 16, J // 16
STEPS = ROWS + CH - 1
LANES = 64
NE, HID = 8, 512
HC = HID // P
SLOT_TILES = NT + NE - 1
PAY = 260
NO_TOKEN = 1 << 20
SLOT_LOADS = [(0, 2), (2, 8), (8, SLOT_TILES)]


def build(nc, x, ctx_rows, ctx_t, qkv_wt, qkv_b, out_wt, out_b, gate_w, gate_b, w1, b1, w2, b2, out):
    with ExitStack() as stack:
        def sb(name, shape, dt=F32):
            return stack.enter_context(nc.sbuf_tensor(name, shape, dt))

        def sem(name):
            return stack.enter_context(nc.semaphore(name))

        early_memory = ExitStack()

        def early(name, shape, dt=F32):
            return early_memory.enter_context(nc.sbuf_tensor(name, shape, dt))

        ident = sb("ident", [P, P])
        ones = sb("ones", [P, P])
        eps_col = sb("eps_col", [P, 1])
        X = sb("X", [P, NT, P])
        stats = sb("stats", [P, 3, NT, 6])
        mean_var = sb("mean_var", [P, 3, NT, 2])
        std = sb("std", [P, 3, NT])
        rstd = sb("rstd", [P, 3, NT])
        X1 = sb("X1", [P, NT, P])
        ctxT = sb("ctxT", [P, T * ROWS])
        ctxTm2 = sb("ctxTm2", [P, T * ROWS])
        ctxr = sb("ctxr", [ROWS, T, P])
        aa = sb("aa", [ROWS, T])
        col2 = sb("col2", [LANES, CW])
        table = sb("table", [ROWS, T, 2, J], I32)
        iota_f = sb("iota_f", [ROWS, J])
        picked = sb("picked", [ROWS, T, 2, ROWS])
        diag = sb("diag", [ROWS, T, 2, ROWS])
        rowsc = sb("rowsc", [ROWS, T, 2])
        upto = sb("upto", [ROWS, T, J])
        onpath = sb("onpath", [ROWS, T, J])
        gw = sb("gw", [P, NE])
        gb = sb("gb", [P, NE])
        W1 = sb("W1", [P, NE, HID])
        W2 = sb("W2", [P, NE, HC, P])
        B2 = sb("B2", [1, NE, P])
        rev_e = sb("rev_e", [P, NE])
        tile_no = sb("tile_no", [P, NE])
        slot_tile = sb("slot_tile", [P, SLOT_TILES])
        token_no = sb("token_no", [P, NT])
        before = sb("before", [P, P], BF16)
        ones_h = sb("ones_h", [P, P], BF16)
        empty = sb("empty", [P, PAY])

        XB = early("XB", [P, NT, P])
        H = early("H", [P, NT, P])
        HT = early("HT", [P, NT * P])
        wqkv = early("wqkv", [P, 3 * P])
        bqkv = early("bqkv", [P, 3 * P])
        wo = early("wo", [P, P])
        bo = early("bo", [P, P])
        QKV = early("QKV", [P, NT, 3 * P])
        dk = early("dk", [P, TPB, P])
        dv = early("dv", [P, TPB, P])
        prod = early("prod", [P, T, TPB, P])
        score = early("score", [P, T, TPB * HEADS])
        dif = early("dif", [P, T, TPB * HEADS])
        dif_hi = early("dif_hi", [P, T, TPB * HEADS])
        dif_lo = early("dif_lo", [P, T, TPB * HEADS])
        exp_old = early("exp_old", [P, T, TPB * HEADS])
        exp_new = early("exp_new", [P, T, TPB * HEADS])
        exp_sum = early("exp_sum", [P, T, TPB * HEADS])
        exp_rec = early("exp_rec", [P, T, TPB * HEADS])
        prob = early("prob", [P, T, TPB * HEADS])
        pdv = early("pdv", [P, T, TPB, P])
        att = early("att", [P, NT, P])
        attT = early("attT", [P, NT * P])
        S = early("S", [P, NT, P])
        ST = early("ST", [P, NT * P])
        SQ = early("SQ", [P, NT * P])
        ctxsq = early("ctxsq", [ROWS, T, P])
        D = early("D", [ROWS, T, J])
        Dsk = early("Dsk", [LANES, STEPS, CW + 1])
        M = early("M", [LANES, STEPS, CW + 1])
        R = early("R", [LANES, STEPS + 1, CW + 1])
        dg = early("dg", [LANES, STEPS, CW], BF16)
        notleft = early("notleft", [LANES, STEPS, CW], BF16)
        V = early("V", [LANES, STEPS, CW])
        Vr = early("Vr", [ROWS, T, J])
        early_memory.close()
        F = sb("F", [P, NT, P])
        FT = sb("FT", [P, NT * P])
        logit = sb("logit", [P, NT, NE])
        lmax = sb("lmax", [P, NT])
        lsh = sb("lsh", [P, NT, NE])
        lexp = sb("lexp", [P, NT, NE])
        lsum = sb("lsum", [P, NT])
        lrec = sb("lrec", [P, NT])
        gs = sb("gs", [P, NT, NE])
        gs2 = sb("gs2", [P, NT, NE])
        top = sb("top", [P, 2, NT])
        hit = sb("hit", [P, 2, NT, NE])
        rev = sb("rev", [P, 2, NT, NE])
        first = sb("first", [P, 2, NT])
        taken = sb("taken", [P, NT, NE])
        absent = sb("absent", [P, NT])
        chosen = sb("chosen", [P, NT])
        onehot = sb("onehot", [P, NT, NE], BF16)
        wsel = sb("wsel", [P, NT, NE])
        wgate = sb("wgate", [P, NT])
        tiles_gt = sb("tiles_gt", [P, NE, NE])
        tiles_of = sb("tiles_of", [P, NE])
        tiles_end = sb("tiles_end", [P, NE])
        base = sb("base", [P, NE])
        place = sb("place", [P, NT, NE])
        place_sel = sb("place_sel", [P, NT, NE])
        slot_f = sb("slot_f", [P, NT])
        slot = sb("slot", [P, NT], U32)
        ended = sb("ended", [P, SLOT_TILES, NE])
        expert_f = sb("expert_f", [P, SLOT_TILES])
        expert = sb("expert", [P, SLOT_TILES], I32)
        pay = sb("pay", [P, NT, PAY])
        XS = sb("XS", [P, SLOT_TILES, PAY])
        token = sb("token", [P, SLOT_TILES], U32)
        B1 = sb("B1", [P, NE, HID])
        XT = sb("XT", [P, 2, P])
        HB = sb("HB", [P, 2, HID])
        HT2 = sb("HT2", [P, 2, HID])
        YS = sb("YS", [P, SLOT_TILES, P])
        banks = [stack.enter_context(nc.psum_tensor(f"bank{i}", [P, 512], F32)) for i in range(8)]
        d_scratch = nc.dram_tensor("d_scratch", (T, CH, STEPS, CW + 1), F32)
        slots_dram = nc.dram_tensor("slots_dram", (SLOT_TILES * P, PAY), F32)
        v_scratch = nc.dram_tensor("v_scratch", (T, CH, STEPS, CW), F32)

        x_in = sem("x_in"); attn_in = sem("attn_in"); ctx_in = sem("ctx_in")
        moe_in = sem("moe_in"); out_done = sem("out_done")
        const_done = sem("const_done"); pool_step = sem("pool_step"); lanes_done = sem("lanes_done")
        dve_step = sem("dve_step"); act_step = sem("act_step")
        var_done = sem("var_done"); std_done = sem("std_done"); norm_done = sem("norm_done")
        tr_done = sem("tr_done"); tr_copied = sem("tr_copied")
        qkv_done = sem("qkv_done"); qkv_copied = sem("qkv_copied")
        xb_done = sem("xb_done"); split_done = sem("split_done"); exp_done = sem("exp_done")
        att_done = sem("att_done"); proj_done = sem("proj_done"); x1_done = sem("x1_done")
        m2_done = sem("m2_done"); sq_done = sem("sq_done"); dist_done = sem("dist_done")
        d2_done = sem("d2_done"); d_done = sem("d_done")
        prefill = sem("prefill"); d_out = sem("d_out"); dsk_in = sem("dsk_in")
        low_done = sem("low_done"); scan_done = sem("scan_done"); mask_done = sem("mask_done")
        v_done = sem("v_done"); v_out = sem("v_out"); v_in = sem("v_in")
        table_done = sem("table_done"); picked0 = sem("picked0"); picked1 = sem("picked1")
        path_done = sem("path_done"); exp2_done = sem("exp2_done"); x2_done = sem("x2_done")
        logit_done = sem("logit_done"); lsh_done = sem("lsh_done"); lexp_done = sem("lexp_done")
        hot_done = sem("hot_done"); fs_done = sem("fs_done")
        hit_done = sem("hit_done"); empties = sem("empties"); expert_done = sem("expert_done")
        count_done = sem("count_done"); pay_done = sem("pay_done"); sent = sem("sent"); slots_in = [sem(f"slots_in{i}") for i in range(len(SLOT_LOADS))]
        token_done = sem("token_done"); xt_done = sem("xt_done"); xt_copied = sem("xt_copied")
        hid_done = sem("hid_done"); hid_biased = sem("hid_biased"); hidT_done = sem("hidT_done")
        hidT_copied = sem("hidT_copied")
        y_done = sem("y_done"); ys_done = sem("ys_done")

        block = stack.enter_context(nc.Block())
        x_v = x.rearrange("t (n p) d -> p (t n) d", p=P)
        out_v = out.rearrange("t (n p) d -> p (t n) d", p=P)
        SK = CW + 1

        @block.sync
        def _(sp):
            sp.dma_start(X[:], x_v).then_inc(x_in, 16)
            sp.dma_start(wqkv[:], qkv_wt).then_inc(attn_in, 16)
            sp.dma_start(bqkv[:], qkv_b.partition_broadcast(P)).then_inc(attn_in, 16)
            sp.dma_start(wo[:], out_wt).then_inc(attn_in, 16)
            sp.dma_start(bo[:], out_b.partition_broadcast(P)).then_inc(attn_in, 16)
            sp.dma_start(ctxT[:], ctx_t).then_inc(ctx_in, 16)
            sp.dma_start(ctxr[:], ctx_rows.rearrange("t r d -> r t d")).then_inc(ctx_in, 16)
            sp.dma_start(gw[:], gate_w).then_inc(moe_in, 16)
            sp.dma_start(gb[:], gate_b.partition_broadcast(P)).then_inc(moe_in, 16)
            sp.dma_start(B2[:], b2.unsqueeze(0)).then_inc(moe_in, 16)
            sp.wait_ge(empties, 1)
            sp.dma_start(slots_dram.ap().rearrange("(k p) f -> p k f", p=P),
                         empty[:].unsqueeze(1).to_broadcast([P, SLOT_TILES, PAY])).then_inc(prefill, 16)
            sp.wait_ge(lanes_done, 1)
            for b in range(T):
                sp.dma_start(d_scratch.ap()[b], Dsk[32 * b:32 * b + CH]).then_inc(prefill, 16)
            sp.dma_start(W1[:], w1.rearrange("e d h -> d e h")).then_inc(moe_in, 16)
            sp.dma_start(W2[:], w2.rearrange("e (c p) d -> p e c d", p=P)).then_inc(moe_in, 16)
            sp.wait_ge(prefill, 48)
            for b in range(T):
                sp.wait_ge(d_done, b + 1)
                dst = bass.AP(d_scratch, b * CH * STEPS * SK + 1, [[SK, ROWS], [STEPS * SK + SK, CH], [1, CW]])
                sp.dma_start(dst, D[:, b, :].rearrange("r (c w) -> r c w", w=CW)).then_inc(d_out, 16)
            sp.wait_ge(d_out, 32)
            for b in range(T):
                sp.dma_start(Dsk[32 * b:32 * b + CH], d_scratch.ap()[b]).then_inc(dsk_in, 16)
            for b in range(T):
                sp.wait_ge(v_done, 1)
                sp.dma_start(v_scratch.ap()[b], V[32 * b:32 * b + CH]).then_inc(v_out, 16)
            sp.wait_ge(v_out, 32)
            for b in range(T):
                src = bass.AP(v_scratch, b * CH * STEPS * CW, [[CW, ROWS], [STEPS * CW + CW, CH], [1, CW]])
                sp.dma_start(Vr[:, b, :].rearrange("r (c w) -> r c w", w=CW), src).then_inc(v_in, 16)
            sp.wait_ge(table_done, 2)
            sp.dma_start(B1[:].rearrange("p e h -> p (e h)"),
                         b1.rearrange("e h -> (e h)").partition_broadcast(P)).then_inc(moe_in, 16)
            sp.wait_ge(sent, 16 * NT)
            slots_v = slots_dram.ap().rearrange("(k p) f -> p k f", p=P)
            for i, (k0, k1) in enumerate(SLOT_LOADS):
                sp.dma_start(XS[:, k0:k1, :], slots_v[:, k0:k1, :]).then_inc(slots_in[i], 16)

        @block.gpsimd
        def _(pool):
            steps = [0]

            def step(i):
                steps[0] += 1
                i.then_inc(pool_step, 1)
                pool.wait_ge(pool_step, steps[0])

            def lanes(b):
                return slice(32 * b, 32 * b + 32)

            step(nc.gpsimd.memset(ident[:], 0.0))
            step(nc.gpsimd.affine_select(out=ident[:], in_=ident[:], pattern=[[-1, P]], compare_op=ALU.not_equal,
                                         fill=1.0, base=0, channel_multiplier=1))
            step(nc.gpsimd.memset(ones[:], 1.0))
            step(nc.gpsimd.memset(eps_col[:], EPS))
            pool.sem_inc(const_done, 1)
            step(nc.gpsimd.memset(Dsk[:], BIG))
            step(nc.gpsimd.memset(Dsk[:, :, 0:1], 0.0))
            step(nc.gpsimd.memset(R[:, 0, :], BIG))
            for b in range(T):
                step(nc.gpsimd.memset(R[32 * b:32 * b + 1, 0, 0:1], 0.0))
            pool.sem_inc(lanes_done, 1)
            for b in range(T):
                step(nc.gpsimd.iota(col2[lanes(b), :], pattern=[[2, CW]], base=0, channel_multiplier=2 * CW,
                                    allow_small_or_imprecise_dtypes=True))
            step(nc.gpsimd.iota(iota_f[:], pattern=[[1, J]], base=0, channel_multiplier=0,
                                allow_small_or_imprecise_dtypes=True))
            for b in range(T):
                step(nc.gpsimd.iota(table[:, b, 1, :], pattern=[[1, J]], base=0, channel_multiplier=0))
            step(nc.gpsimd.iota(rev_e[:], pattern=[[-1, NE]], base=NE, channel_multiplier=0,
                                allow_small_or_imprecise_dtypes=True))
            step(nc.gpsimd.iota(tile_no[:], pattern=[[P, NE]], base=0, channel_multiplier=0,
                                allow_small_or_imprecise_dtypes=True))
            step(nc.gpsimd.iota(slot_tile[:], pattern=[[1, SLOT_TILES]], base=0, channel_multiplier=0,
                                allow_small_or_imprecise_dtypes=True))
            step(nc.gpsimd.iota(token_no[:], pattern=[[P, NT]], base=0, channel_multiplier=1,
                                allow_small_or_imprecise_dtypes=True))
            step(nc.gpsimd.memset(ones_h[:], 1.0))
            step(nc.gpsimd.affine_select(out=before[:], in_=ones_h[:], pattern=[[1, P]],
                                         compare_op=ALU.is_gt, fill=0.0, base=0, channel_multiplier=-1))
            step(nc.gpsimd.memset(empty[:], 0.0))
            step(nc.gpsimd.memset(empty[:, 2 * P:], float(NO_TOKEN)))
            pool.sem_inc(empties, 1)
            pool.sem_inc(const_done, 1)
            pool.wait_ge(x_in, 16)
            pool.wait_ge(attn_in, 64)
            step(nc.gpsimd.tensor_tensor(XB[:], X[:], bo[:].unsqueeze(1).to_broadcast([P, NT, P]), ALU.add))
            pool.sem_inc(xb_done, 1)
            pool.wait_ge(mask_done, 2 * STEPS)
            step(nc.gpsimd.tensor_tensor(V[:], col2[:].unsqueeze(1).to_broadcast([LANES, STEPS, CW]), dg[:],
                                         ALU.subtract))
            step(nc.gpsimd.tensor_tensor(V[:], V[:], notleft[:], ALU.mult))
            pool.sem_inc(v_done, 1)
            pool.wait_ge(prefill, 48)
            for n in range(NT):
                pool.wait_ge(pay_done, n + 1)
                nc.gpsimd.indirect_dma_start(
                    out=slots_dram.ap(), out_offset=bass.IndirectOffsetOnAxis(slot[:, n:n + 1], 0),
                    in_=pay[:, n, :], in_offset=None, bounds_check=SLOT_TILES * P - 1,
                    oob_is_err=False).then_inc(sent, 16)
            for k in range(SLOT_TILES):
                pool.wait_ge(token_done, k + 1)
                pool.wait_ge(ys_done, k + 1)
                nc.gpsimd.indirect_dma_start(
                    out=out.rearrange("t j d -> (t j) d"),
                    out_offset=bass.IndirectOffsetOnAxis(token[:, k:k + 1], 0),
                    in_=YS[:, k, :], in_offset=None, bounds_check=T * J - 1,
                    oob_is_err=False).then_inc(out_done, 16)
            pool.wait_ge(out_done, 16 * SLOT_TILES)

        def follow_path(eng, copy, b, done):
            eng.wait_ge(table_done, b + 1)
            eng.wait_ge(const_done, 2)
            col = J - 1
            for i in range(ROWS - 1, -1, -1):
                copy(picked[:, b, :, i], table[:, b, :, bass.ds(col, 1)].squeeze(2)).then_inc(done, 1)
                if i:
                    code = eng.value_load(table[i:i + 1, b, 0, bass.ds(col, 1)])
                    col = nc.s_assert_within(code // 2, 0, J - 1, skip_runtime_bounds_check_because=
                                             "a code is twice a column of the row, or one less")

        def expert_of(eng, k):
            return nc.s_assert_within(eng.value_load(expert[0:1, k:k + 1]), 0, NE - 1,
                                      skip_runtime_bounds_check_because="the last expert is the largest number")

        @block.vector
        def _(dve):
            steps = [0]

            def step(i):
                steps[0] += 1
                i.then_inc(dve_step, 1)
                dve.wait_ge(dve_step, steps[0])

            def norm(k, src, dst, ready, need):
                dve.wait_ge(ready, need)
                for n in range(NT):
                    i = nc.vector.bn_stats(stats[:, k, n, :], src[:, n, :])
                step(i)
                for n in range(NT):
                    i = nc.vector.bn_aggr(mean_var[:, k, n, :], stats[:, k, n, :])
                i.then_inc(var_done, 1)
                dve.wait_ge(std_done, k + 1)
                step(nc.vector.reciprocal(rstd[:, k, :], std[:, k, :]))
                for n in range(NT):
                    i = nc.vector.tensor_scalar(dst[:, n, :], src[:, n, :], mean_var[:, k, n, 0:1],
                                                rstd[:, k, n:n + 1], ALU.subtract, ALU.mult)
                i.then_inc(norm_done, 1)

            norm(0, X, H, x_in, 16)
            dve.wait_ge(attn_in, 64)
            for n in range(NT):
                dve.wait_ge(qkv_done, n + 1)
                nc.vector.tensor_tensor(QKV[:, n, :], banks[(n + 2) % 8][:, 0:3 * P], bqkv[:],
                                        ALU.add).then_inc(qkv_copied, 1)
            dve.wait_ge(qkv_copied, NT)
            q, k, v = (QKV[:, :, i * P:(i + 1) * P] for i in range(3))
            t0, t1 = slice(0, TPB), slice(TPB, NT)
            nc.vector.tensor_tensor(prod[:, 0], q[:, t0, :], k[:, t0, :], ALU.mult)
            step(nc.vector.tensor_tensor(dk[:], k[:, t1, :], k[:, t0, :], ALU.subtract))
            nc.vector.tensor_tensor(dv[:], v[:, t1, :], v[:, t0, :], ALU.subtract)
            step(nc.vector.tensor_tensor(prod[:, 1], q[:, t1, :], dk[:], ALU.mult))
            step(nc.vector.tensor_reduce(score[:], prod[:].rearrange("p t n (h d) -> p t (n h) d", d=DH),
                                         AX_X, ALU.add))
            nc.vector.tensor_scalar(dif[:, 0], score[:, 0], -(DH ** -0.5), MASKED, ALU.mult, ALU.add)
            step(nc.vector.tensor_scalar(dif[:, 1], score[:, 1], DH ** -0.5, None, ALU.mult))
            nc.vector.tensor_scalar(dif_hi[:], dif[:], 0.0, None, ALU.max)
            nc.vector.tensor_scalar(dif_lo[:], dif[:], 0.0, None, ALU.min).then_inc(split_done, 1)
            dve.wait_ge(exp_done, 2)
            step(nc.vector.tensor_tensor(exp_sum[:], exp_old[:], exp_new[:], ALU.add))
            step(nc.vector.reciprocal(exp_rec[:], exp_sum[:]))
            step(nc.vector.tensor_tensor(prob[:], exp_new[:], exp_rec[:], ALU.mult))
            for t in range(T):
                i = nc.vector.tensor_tensor(
                    pdv[:, t].rearrange("p n (h d) -> p (n h) d", d=DH),
                    prob[:, t].unsqueeze(2).to_broadcast([P, TPB * HEADS, DH]),
                    dv[:].rearrange("p n (h d) -> p (n h) d", d=DH), ALU.mult)
            step(i)
            for t in range(T):
                i = nc.vector.tensor_tensor(att[:, t * TPB:(t + 1) * TPB, :], pdv[:, t], v[:, t0, :], ALU.add)
            i.then_inc(att_done, 1)
            dve.wait_ge(xb_done, 1)
            for t in range(T):
                dve.wait_ge(proj_done, t + 1)
                nc.vector.tensor_tensor(X1[:, t * TPB:(t + 1) * TPB, :],
                                        banks[4 + t][:].rearrange("p (n d) -> p n d", d=P),
                                        XB[:, t * TPB:(t + 1) * TPB, :], ALU.add).then_inc(x1_done, 1)
            norm(1, X1, S, x1_done, 2)
            dve.wait_ge(ctx_in, 32)
            nc.vector.tensor_scalar(ctxTm2[:], ctxT[:], -2.0, None, ALU.mult).then_inc(m2_done, 1)
            step(nc.vector.tensor_tensor(ctxsq[:], ctxr[:], ctxr[:], ALU.mult))
            step(nc.vector.tensor_reduce(aa[:], ctxsq[:], AX_X, ALU.add))
            for b in range(T):
                dve.wait_ge(dist_done, b + 1)
                nc.vector.tensor_scalar(D[:, b, :], banks[b][0:ROWS, :], aa[:, b:b + 1], 0.0, ALU.add,
                                        ALU.max).then_inc(d2_done, 1)

            shift = [CH] + list(range(CH - 1)) + [CH] + list(range(CH, 31))
            dve.wait_ge(lanes_done, 1)
            dve.wait_ge(dsk_in, 32)
            for s in range(STEPS):
                if s:
                    dve.wait_ge(scan_done, s)
                nc.vector.tensor_tensor(M[:, s, 1:SK], R[:, s, 1:SK], R[:, s, 0:CW], ALU.min).then_inc(low_done, 1)
                nc.vector.stream_shuffle(M[:, s, 0:1], R[:, s, CW:SK], shift).then_inc(low_done, 1)
                nc.vector.tensor_tensor(dg[:, s, :], R[:, s, 0:CW], R[:, s, 1:SK], ALU.is_le).then_inc(mask_done, 1)
                dve.wait_ge(low_done, 2 * s + 2)
                nc.vector.tensor_tensor_scan(R[:, s + 1, :], M[:, s, :], Dsk[:, s, :], BIG, ALU.min,
                                             ALU.add).then_inc(scan_done, 1)
                if s:
                    nc.vector.tensor_tensor(notleft[:, s - 1, :], R[:, s, 0:CW], M[:, s - 1, 1:SK],
                                            ALU.is_ge).then_inc(mask_done, 1)
            dve.wait_ge(scan_done, STEPS)
            nc.vector.tensor_tensor(notleft[:, STEPS - 1, :], R[:, STEPS, 0:CW], M[:, STEPS - 1, 1:SK],
                                    ALU.is_ge).then_inc(mask_done, 1)
            dve.wait_ge(v_in, 32)
            for b in range(T):
                nc.vector.tensor_tensor_scan(table[:, b, 0, :], Vr[:, b, :], Vr[:, b, :], 0.0, ALU.max,
                                             ALU.max).then_inc(table_done, 1)
            follow_path(dve, nc.vector.tensor_copy, 1, picked1)

            dve.wait_ge(picked0, ROWS)
            dve.wait_ge(picked1, ROWS)
            step(nc.vector.tensor_tensor(diag[:].rearrange("r b q i -> r (b q) i"),
                                         picked[:].rearrange("r b q i -> r (b q) i"),
                                         ident[0:ROWS, 0:ROWS].unsqueeze(1).to_broadcast([ROWS, 2 * T, ROWS]), ALU.mult))
            step(nc.vector.tensor_reduce(rowsc[:], diag[:], AX_X, ALU.add))
            for b in range(T):
                i = nc.vector.tensor_scalar(upto[:, b, :], iota_f[:], rowsc[:, b, 1:2], None, ALU.is_le)
            step(i)
            for b in range(T):
                nc.vector.scalar_tensor_tensor(out=onpath[:, b, :], in0=table[:, b, 0, :], scalar=rowsc[:, b, 0:1],
                                               in1=upto[:, b, :], op0=ALU.is_equal,
                                               op1=ALU.mult).then_inc(path_done, 1)
            for b in range(T):
                dve.wait_ge(exp2_done, b + 1)
                nc.vector.tensor_tensor(pay[:, b * TPB:(b + 1) * TPB, P:2 * P],
                                        banks[2 + b][:].rearrange("p (n d) -> p n d", d=P),
                                        X1[:, b * TPB:(b + 1) * TPB, :], ALU.add).then_inc(x2_done, 1)
            X2 = pay[:, :, P:2 * P]
            norm(2, X2, F, x2_done, 2)

            dve.wait_ge(const_done, 2)
            dve.wait_ge(moe_in, 96)
            dve.wait_ge(logit_done, 1)
            step(nc.vector.tensor_tensor(logit[:], banks[6][:, 0:NT * NE].rearrange("p (n e) -> p n e", e=NE),
                                         gb[:].unsqueeze(1).to_broadcast([P, NT, NE]), ALU.add))
            step(nc.vector.tensor_reduce(lmax[:], logit[:], AX_X, ALU.max))
            nc.vector.tensor_tensor(lsh[:], logit[:], lmax[:].unsqueeze(2).to_broadcast([P, NT, NE]),
                                    ALU.subtract).then_inc(lsh_done, 1)
            dve.wait_ge(lexp_done, 1)
            step(nc.vector.tensor_reduce(lsum[:], lexp[:], AX_X, ALU.add))
            step(nc.vector.reciprocal(lrec[:], lsum[:]))
            step(nc.vector.tensor_tensor(gs[:], lexp[:], lrec[:].unsqueeze(2).to_broadcast([P, NT, NE]), ALU.mult))
            def spread(col):
                return col.unsqueeze(2).to_broadcast([P, NT, NE])

            rev_b = rev_e[:].unsqueeze(1).to_broadcast([P, NT, NE])
            for r, left in ((0, gs), (1, gs2)):
                step(nc.vector.tensor_reduce(top[:, r], left[:], AX_X, ALU.max))
                step(nc.vector.tensor_tensor(hit[:, r], left[:], spread(top[:, r]), ALU.is_equal))
                step(nc.vector.tensor_tensor(rev[:, r], hit[:, r], rev_b, ALU.mult))
                step(nc.vector.tensor_reduce(first[:, r], rev[:, r], AX_X, ALU.max))
                if r == 0:
                    step(nc.vector.tensor_tensor(taken[:], rev_b, spread(first[:, 0]), ALU.is_equal))
                    step(nc.vector.scalar_tensor_tensor(out=gs2[:], in0=taken[:], scalar=-2.0, in1=gs[:],
                                                        op0=ALU.mult, op1=ALU.add))
            step(nc.vector.tensor_scalar(absent[:], top[:, 1], 0.0, float(NE), ALU.is_le, ALU.mult))
            step(nc.vector.tensor_tensor(absent[:], absent[:], first[:, 1], ALU.add))
            step(nc.vector.tensor_tensor(chosen[:], absent[:], first[:, 0], ALU.min))
            nc.vector.tensor_tensor(onehot[:], rev_b, spread(chosen[:]), ALU.is_equal).then_inc(hit_done, 1)
            dve.wait_ge(hit_done, 1)
            step(nc.vector.tensor_tensor(wsel[:], onehot[:], gs[:], ALU.mult))
            step(nc.vector.tensor_reduce(wgate[:], wsel[:], AX_X, ALU.add))
            for n in range(NT):
                nc.vector.tensor_scalar(pay[:, n, 0:P], F[:, n, :], wgate[:, n:n + 1], None, ALU.mult)
            nc.vector.tensor_copy(pay[:, :, 2 * P:].rearrange("p n f -> p n f"),
                                  token_no[:].unsqueeze(2).to_broadcast([P, NT, PAY - 2 * P]))
            dve.wait_ge(count_done, 2)
            step(nc.vector.tensor_tensor(tiles_gt[:], banks[7][:, 0:NE].unsqueeze(2).to_broadcast([P, NE, NE]),
                                         tile_no[:].unsqueeze(1).to_broadcast([P, NE, NE]), ALU.is_gt))
            step(nc.vector.tensor_reduce(tiles_of[:], tiles_gt[:], AX_X, ALU.add))
            step(nc.vector.tensor_tensor_scan(tiles_end[:], ones[:, 0:NE], tiles_of[:], 0.0, ALU.mult, ALU.add))
            step(nc.vector.tensor_tensor(base[:], tiles_end[:], tiles_of[:], ALU.subtract))
            step(nc.vector.tensor_scalar(base[:], base[:], float(P), None, ALU.mult))
            step(nc.vector.tensor_tensor(place[:], banks[6][:, NT * NE:2 * NT * NE].rearrange("p (n e) -> p n e", e=NE),
                                         base[:].unsqueeze(1).to_broadcast([P, NT, NE]), ALU.add))
            step(nc.vector.tensor_tensor(place_sel[:], place[:], onehot[:], ALU.mult))
            step(nc.vector.tensor_reduce(slot_f[:], place_sel[:], AX_X, ALU.add))
            nc.vector.tensor_copy(slot[:], slot_f[:]).then_inc(pay_done, NT)
            step(nc.vector.tensor_tensor(ended[:], tiles_end[:].unsqueeze(1).to_broadcast([P, SLOT_TILES, NE]),
                                         slot_tile[:].unsqueeze(2).to_broadcast([P, SLOT_TILES, NE]), ALU.is_le))
            step(nc.vector.tensor_reduce(expert_f[:], ended[:], AX_X, ALU.add))
            nc.vector.tensor_scalar(expert[:], expert_f[:], float(NE - 1), None, ALU.min).then_inc(expert_done, 1)
            dve.wait_ge(expert_done, 1)
            for k in range(SLOT_TILES + 2):
                if k < SLOT_TILES:
                    if k in [k0 for k0, _ in SLOT_LOADS]:
                        i = [k0 for k0, _ in SLOT_LOADS].index(k)
                        k1 = SLOT_LOADS[i][1]
                        dve.wait_ge(slots_in[i], 16)
                        nc.vector.tensor_copy(token[:, k:k1], XS[:, k:k1, 2 * P]).then_inc(token_done, k1 - k)
                    e = expert_of(dve, k)
                    dve.wait_ge(hid_done, k + 1)
                    if k >= 2:
                        dve.wait_ge(hidT_done, k - 1)
                    nc.vector.tensor_tensor(HB[:, k % 2, :], banks[2 + k % 2][:],
                                            B1[:, bass.ds(e, 1), :].squeeze(1), ALU.add).then_inc(hid_biased, 1)
                if k >= 2:
                    dve.wait_ge(y_done, k - 1)
                    nc.vector.tensor_tensor(YS[:, k - 2, :], banks[6 + k % 2][:, 0:P], XS[:, k - 2, P:2 * P],
                                            ALU.add).then_inc(ys_done, 1)

        @block.scalar
        def _(act):
            act.wait_ge(const_done, 1)

            def root(k):
                act.wait_ge(var_done, k + 1)
                nc.scalar.activation(std[:, k, :], mean_var[:, k, :, 1], ACT.Sqrt, bias=eps_col[:]).then_inc(std_done, 1)

            def copy_t(dst, first_bank, count):
                for t in range(T):
                    act.wait_ge(tr_done, count + t + 1)
                    nc.scalar.copy(dst[:, t * J:(t + 1) * J], banks[first_bank + t][:]).then_inc(tr_copied, 1)

            root(0)
            copy_t(HT, 0, 0)
            act.wait_ge(split_done, 1)
            nc.scalar.activation(exp_old[:], dif_hi[:], ACT.Exp, scale=-1.0).then_inc(exp_done, 1)
            nc.scalar.activation(exp_new[:], dif_lo[:], ACT.Exp).then_inc(exp_done, 1)
            copy_t(attT, 2, 2)
            root(1)
            for t in range(T):
                act.wait_ge(tr_done, 4 + t + 1)
                nc.scalar.copy(ST[:, t * J:(t + 1) * J], banks[6 + t][:]).then_inc(tr_copied, 1)
                nc.scalar.activation(SQ[:, t * J:(t + 1) * J], banks[6 + t][:], ACT.Square).then_inc(sq_done, 1)
            for b in range(T):
                act.wait_ge(d2_done, b + 1)
                nc.scalar.activation(D[:, b, :], D[:, b, :], ACT.Sqrt).then_inc(d_done, 1)
            follow_path(act, nc.scalar.copy, 0, picked0)
            root(2)
            copy_t(FT, 4, 6)
            act.wait_ge(lsh_done, 1)
            nc.scalar.activation(lexp[:], lsh[:], ACT.Exp).then_inc(lexp_done, 1)
            for k in range(SLOT_TILES + 1):
                if k < SLOT_TILES:
                    act.wait_ge(xt_done, k + 1)
                    if k >= 2:
                        act.wait_ge(hid_done, k - 1)
                    nc.scalar.copy(XT[:, k % 2, :], banks[k % 2][:, 0:P]).then_inc(xt_copied, 1)
                if k:
                    act.wait_ge(hidT_done, k)
                    if k >= 3:
                        act.wait_ge(y_done, k - 2)
                    nc.scalar.activation(HT2[:, (k - 1) % 2, :], banks[4 + (k - 1) % 2][:],
                                         ACT.Relu).then_inc(hidT_copied, 1)

        @block.tensor
        def _(pe):
            pe.wait_ge(const_done, 1)

            def transposes(src, first_bank, only_half=None):
                for n in range(NT):
                    i = nc.tensor.transpose(banks[first_bank + n // TPB][:, (n % TPB) * P:(n % TPB + 1) * P],
                                            src[:, n, :], ident[:])
                    if n % TPB == TPB - 1:
                        i.then_inc(tr_done, 1)

            pe.wait_ge(norm_done, 1)
            transposes(H, 0)
            pe.wait_ge(attn_in, 64)
            pe.wait_ge(tr_copied, 2)
            for n in range(NT):
                nc.tensor.matmul(banks[(n + 2) % 8][:, 0:3 * P], HT[:, n * P:(n + 1) * P], wqkv[:],
                                 start=True, stop=True).then_inc(qkv_done, 1)
            pe.wait_ge(att_done, 1)
            transposes(att, 2)
            pe.wait_ge(tr_copied, 4)
            for n in range(NT):
                i = nc.tensor.matmul(banks[4 + n // TPB][:, (n % TPB) * P:(n % TPB + 1) * P],
                                     attT[:, n * P:(n + 1) * P], wo[:], start=True, stop=True)
                if n % TPB == TPB - 1:
                    i.then_inc(proj_done, 1)
            pe.wait_ge(norm_done, 2)
            transposes(S, 6)
            pe.wait_ge(m2_done, 1)
            for b in range(T):
                pe.wait_ge(sq_done, b + 1)
                nc.tensor.matmul(banks[b][0:ROWS, :], ones[:, 0:ROWS], SQ[:, b * J:(b + 1) * J], start=True, stop=False)
                nc.tensor.matmul(banks[b][0:ROWS, :], ctxTm2[:, b * ROWS:(b + 1) * ROWS], ST[:, b * J:(b + 1) * J],
                                 start=False, stop=True).then_inc(dist_done, 1)
            for b in range(T):
                pe.wait_ge(path_done, b + 1)
                for n in range(TPB):
                    i = nc.tensor.matmul(banks[2 + b][:, n * P:(n + 1) * P], onpath[:, b, n * P:(n + 1) * P],
                                         ctxr[:, b, :], start=True, stop=True)
                i.then_inc(exp2_done, 1)
            pe.wait_ge(norm_done, 3)
            transposes(F, 4)
            pe.wait_ge(tr_copied, 8)
            pe.wait_ge(moe_in, 96)
            for n in range(NT):
                i = nc.tensor.matmul(banks[6][:, n * NE:(n + 1) * NE], FT[:, n * P:(n + 1) * P], gw[:],
                                     start=True, stop=True)
            i.then_inc(logit_done, 1)
            pe.wait_ge(hit_done, 1)
            places = banks[6][:, NT * NE:2 * NT * NE]
            hot = onehot[:].rearrange("p n e -> p (n e)")
            nc.tensor.matmul(places, before[:], hot, start=True, stop=False)
            for n in range(NT - 1):
                i = nc.tensor.matmul(places[:, (n + 1) * NE:], ones_h[:],
                                     onehot[:, n:n + 1, :].to_broadcast([P, NT - 1 - n, NE]),
                                     start=False, stop=(n == NT - 2))
            i.then_inc(count_done, 1)
            for n in range(NT):
                i = nc.tensor.matmul(banks[7][:, 0:NE], ones_h[:], onehot[:, n, :], start=(n == 0), stop=(n == NT - 1))
            i.then_inc(count_done, 1)
            pe.wait_ge(expert_done, 1)

            def turn_input(k):
                if k in [k0 for k0, _ in SLOT_LOADS]:
                    pe.wait_ge(slots_in[[k0 for k0, _ in SLOT_LOADS].index(k)], 16)
                if k >= 2:
                    pe.wait_ge(xt_copied, k - 1)
                nc.tensor.transpose(banks[k % 2][:, 0:P], XS[:, k, 0:P], ident[:]).then_inc(xt_done, 1)

            def hidden(k):
                e = expert_of(pe, k)
                pe.wait_ge(xt_copied, k + 1)
                if k >= 2:
                    pe.wait_ge(hid_biased, k - 1)
                nc.tensor.matmul(banks[2 + k % 2][:], XT[:, k % 2, :], W1[:, bass.ds(e, 1), :].squeeze(1),
                                 start=True, stop=True).then_inc(hid_done, 1)

            def turn_hidden(k):
                pe.wait_ge(hid_biased, k + 1)
                if k >= 2:
                    pe.wait_ge(hidT_copied, k - 1)
                for c in range(HC):
                    i = nc.tensor.transpose(banks[4 + k % 2][:, c * P:(c + 1) * P], HB[:, k % 2, c * P:(c + 1) * P],
                                            ident[:])
                i.then_inc(hidT_done, 1)

            def output(k):
                e = expert_of(pe, k)
                pe.wait_ge(hidT_copied, k + 1)
                if k >= 2:
                    pe.wait_ge(ys_done, k - 1)
                for c in range(HC):
                    nc.tensor.matmul(banks[6 + k % 2][:, 0:P], HT2[:, k % 2, c * P:(c + 1) * P],
                                     W2[:, bass.ds(e, 1), c, :].squeeze(1), start=(c == 0), stop=False)
                nc.tensor.matmul(banks[6 + k % 2][:, 0:P], ones[0:1, :], B2[:, bass.ds(e, 1), :].squeeze(1),
                                 start=False, stop=True).then_inc(y_done, 1)

            turn_input(0)
            for k in range(SLOT_TILES + 2):
                if k + 1 < SLOT_TILES:
                    turn_input(k + 1)
                if k < SLOT_TILES:
                    hidden(k)
                if 1 <= k <= SLOT_TILES:
                    turn_hidden(k - 1)
                if k >= 2:
                    output(k - 2)


def kernel(x, ctx_1024, L0_attn_qkv_w, L0_attn_qkv_b, L0_attn_out_w, L0_attn_out_b, L0_ffn_gate_w,
           L0_ffn_gate_b, L0_ffn_w1, L0_ffn_b1, L0_ffn_w2, L0_ffn_b2):
    import numpy as np
    import concourse.bacc as bacc
    from concourse import mybir
    from concourse.bass_utils import run_bass_kernel_spmd

    nc = bacc.Bacc("TRN2", target_bir_lowering=False, num_devices=1)
    given = {
        "x": x, "ctx_rows": ctx_1024,
        "ctx_t": np.transpose(np.asarray(ctx_1024), (2, 0, 1)).reshape(128, -1),
        "qkv_wt": np.transpose(np.asarray(L0_attn_qkv_w)), "qkv_b": L0_attn_qkv_b,
        "out_wt": np.transpose(np.asarray(L0_attn_out_w)), "out_b": L0_attn_out_b,
        "gate_w": L0_ffn_gate_w, "gate_b": L0_ffn_gate_b,
        "w1": L0_ffn_w1, "b1": L0_ffn_b1, "w2": L0_ffn_w2, "b2": L0_ffn_b2,
    }
    arrays, aps = {}, {}
    for name, a in given.items():
        a = np.ascontiguousarray(a)
        arrays["in_" + name] = a
        aps[name] = nc.dram_tensor("in_" + name, a.shape, mybir.dt.from_np(a.dtype), kind="ExternalInput").ap()
    out = nc.dram_tensor("out_0", (2, 512, 128), mybir.dt.float32, kind="ExternalOutput").ap()
    build(nc, out=out, **aps)
    r = run_bass_kernel_spmd(nc, [arrays], core_ids=[0])
    return r.results[0]["out_0"]
```

```python
from contextlib import ExitStack

import concourse.bass as bass
from concourse import mybir

F32 = mybir.dt.float32
I32 = mybir.dt.int32
U32 = mybir.dt.uint32
BF16 = mybir.dt.bfloat16
F16 = mybir.dt.float16
ALU = mybir.AluOpType
ACT = mybir.ActivationFunctionType
AX_X = mybir.AxisListType.X

P = 128
T, J = 2, 512
NT = T * J // P
TPB = J // P
HEADS, DH = 16, 8
MASKED = -10000.0
EPS = 1e-5
ROWS = 77
BIG = 1e30
CH, CW = 16, J // 16
STEPS = ROWS + CH - 1
LANES = T * CH
SK_ROWS = STEPS + CH - 1
PITCH = T * J
LANE_STRIDE = PITCH - CW
SK_SIZE = SK_ROWS * PITCH + (T - 1) * CH * LANE_STRIDE
KB = 3
NB = -(-ROWS // KB)
PAD = NB * KB - ROWS
BP = T * 32
NE, HID = 8, 512
HC = HID // P
SLOT_TILES = NT + NE - 1
ROW = P + 2
AHEAD = 8
NO_TOKEN = 1 << 20
DIST_PARTS = [(0, 12), (12, STEPS)]
CODE_PARTS = [(0, 47), (47, 68), (68, 80), (80, STEPS)]
WARM_START, WARM_ATTENTION, WARM_NORM, WARM_PATH, WARM_PLACES, WARM_EXPERTS = 3, 29, 14, 42, 2, 11


def build(nc, x, ctx_rows, ctx_t, qkv_wt, qkv_b, out_wt, out_b, gate_w, gate_b, w1, b1_t, w2, b2, out):
    with ExitStack() as stack:
        def sb(name, shape, dt=F32):
            return stack.enter_context(nc.sbuf_tensor(name, shape, dt))

        def sem(name):
            return stack.enter_context(nc.semaphore(name))

        mid_memory, early_memory, path_memory = ExitStack(), ExitStack(), ExitStack()

        def mid(name, shape, dt=F32):
            return mid_memory.enter_context(nc.sbuf_tensor(name, shape, dt))

        def early(name, shape, dt=F32):
            return early_memory.enter_context(nc.sbuf_tensor(name, shape, dt))

        def path(name, shape, dt=F32):
            return path_memory.enter_context(nc.sbuf_tensor(name, shape, dt))

        ident = sb("ident", [P, P])
        ones = sb("ones", [P, P])
        eps_col = sb("eps_col", [P, 1])
        root_of_eps = sb("root_of_eps", [P, 1])
        X = sb("X", [P, NT, P])
        stats = sb("stats", [P, 3, NT, 6])
        mean_var = sb("mean_var", [P, 3, NT, 2])
        std = sb("std", [P, 3, NT])
        rstd = sb("rstd", [P, 3, NT])
        X1 = sb("X1", [P, NT, P])
        ctxT = sb("ctxT", [P, T, PAD + ROWS])
        ctxTm2 = sb("ctxTm2", [P, T * ROWS])
        ctxr = sb("ctxr", [ROWS, T, P])
        ctxb = sb("ctxb", [BP, KB, P + NE])
        aa = sb("aa", [ROWS, T])
        col2 = sb("col2", [LANES, CW], F16)
        next_batch = sb("next_batch", [LANES, CW], F16)
        gw = sb("gw", [P, NE])
        gb = sb("gb", [P, NE])
        W1 = sb("W1", [P, NE, HID])
        W2 = sb("W2", [P, NE, HC, P])
        B1 = sb("B1", [P, NE, HC])
        B2 = sb("B2", [P, NE, P])
        big_rows = sb("big_rows", [CH - 1, T, J])
        zero_row = sb("zero_row", [PAD, T, J], F16)
        rev_e = sb("rev_e", [P, NE])
        codes = sb("codes", [P, J + 1], F16)
        odd_codes = sb("odd_codes", [BP, J], F16)
        block_diag = sb("block_diag", [BP, NB])
        center = sb("center", [P, P])
        X1T = sb("X1T", [P, NT * P])
        ctxb_rest = sb("ctxb_rest", [BP, KB, P + NE])
        ctxb_part = sb("ctxb_part", [BP, KB, 3, P + NE], BF16)
        carry = sb("carry", [P, P + NE])
        tile_no = sb("tile_no", [P, NE])
        slot_tile = sb("slot_tile", [P, SLOT_TILES])
        token_tile = sb("token_tile", [P, NT])
        part_no = sb("part_no", [P, 1])
        slot_no_f = sb("slot_no_f", [P, P])
        slot_no = sb("slot_no", [P, P], BF16)
        before = sb("before", [P, P], BF16)
        ones_h = sb("ones_h", [P, P], BF16)

        Dsk = mid("Dsk", [LANES, STEPS, CW + 1])
        M = mid("M", [LANES, STEPS, CW + 1])
        R = mid("R", [LANES, STEPS + 1, CW + 1])
        dg = mid("dg", [LANES, STEPS, CW], F16)
        notleft = mid("notleft", [LANES, STEPS, CW], F16)
        V = mid("V", [LANES, STEPS, CW], F16)
        SQ = mid("SQ", [P, NT * P])
        S = mid("S", [P, NT, P])
        ST = mid("ST", [P, NT * P])
        D = mid("D", [ROWS, T, J])
        ctxsq = mid("ctxsq", [ROWS, T, P])
        XB = early("XB", [P, NT, P])
        XTT = early("XTT", [P, NT * P])
        wc = early("wc", [P, 3 * P])
        wqkv = early("wqkv", [P, 3 * P])
        bqkv = early("bqkv", [P, 3 * P])
        wo = early("wo", [P, P])
        bo = early("bo", [P, P])
        QKV = early("QKV", [P, NT, 3 * P])
        dk = early("dk", [P, TPB, P])
        dv = early("dv", [P, TPB, P])
        prod = early("prod", [P, T, TPB, P])
        score = early("score", [P, T, TPB * HEADS])
        dif = early("dif", [P, TPB * HEADS])
        dif_hi = early("dif_hi", [P, T, TPB * HEADS])
        dif_lo = early("dif_lo", [P, T, TPB * HEADS])
        exp_old = early("exp_old", [P, T, TPB * HEADS])
        exp_new = early("exp_new", [P, T, TPB * HEADS])
        exp_sum = early("exp_sum", [P, T, TPB * HEADS])
        exp_rec = early("exp_rec", [P, T, TPB * HEADS])
        prob = early("prob", [P, T, TPB * HEADS])
        pdv = early("pdv", [P, T, TPB, P])
        att = early("att", [P, NT, P])
        attT = early("attT", [P, NT * P])
        early_memory.close()
        VB = path("VB", [BP, KB, J], F16)
        code = path("code", [BP, KB, J], F16)
        jump = path("jump", [BP, KB, J], F16)
        exit_up = path("exit_up", [BP, KB - 1, J], F16)
        exit_dia = path("exit_dia", [BP, KB - 1, J], F16)
        up_part = path("up_part", [BP, J], F16)
        diag_part = path("diag_part", [BP, J], F16)
        comp = path("comp", [BP, KB - 2, J], F16)
        block_table = path("block_table", [BP, J + 1], I32)
        picked = path("picked", [BP, NB])
        diag = path("diag", [BP, NB])
        entry = path("entry", [BP, KB + 1])
        crossed = path("crossed", [BP, KB, J], F16)
        upto = path("upto", [BP, KB, J], F16)
        onpath = path("onpath", [BP, KB, J], BF16)
        path_memory.close()
        mid_memory.close()
        G = sb("G", [P, NT, NE])
        logit = sb("logit", [P, NT, NE])
        lmax = sb("lmax", [P, NT])
        lsh = sb("lsh", [P, NT, NE])
        lexp = sb("lexp", [P, NT, NE])
        lsum = sb("lsum", [P, NT])
        lrec = sb("lrec", [P, NT])
        gs = sb("gs", [P, NT, NE])
        gs2 = sb("gs2", [P, NT, NE])
        top = sb("top", [P, 2, NT])
        hit = sb("hit", [P, 2, NT, NE])
        rev = sb("rev", [P, 2, NT, NE])
        first = sb("first", [P, 2, NT])
        taken = sb("taken", [P, NT, NE])
        absent = sb("absent", [P, NT])
        chosen = sb("chosen", [P, NT])
        onehot = sb("onehot", [P, NT, NE], BF16)
        wsel = sb("wsel", [P, NT, NE])
        wgate = sb("wgate", [P, NT])
        tiles_gt = sb("tiles_gt", [P, NE, NE])
        tiles_of = sb("tiles_of", [P, NE])
        ends = sb("ends", [P, NE + 1])
        rank_sel = sb("rank_sel", [P, NT, NE])
        rank_f = sb("rank_f", [P, NT])
        base_sel = sb("base_sel", [P, NT, NE])
        base_f = sb("base_f", [P, NT])
        tile_f = sb("tile_f", [P, NT])
        ended = sb("ended", [P, SLOT_TILES, NE])
        expert_f = sb("expert_f", [P, SLOT_TILES])
        expert = sb("expert", [P, SLOT_TILES], I32)
        X2 = sb("X2", [P, NT, P])
        norm_gate = sb("norm_gate", [P, NT, 2])
        reached = sb("reached", [P, NT, NE - 1])
        in_tile = sb("in_tile", [P, NT, SLOT_TILES])
        full_tiles = sb("full_tiles", [P, NT])
        within = sb("within", [P, NT])
        at_slot = sb("at_slot", [P, NT, P], BF16)
        number = sb("number", [P, NT, SLOT_TILES, 2], BF16)
        slot_token = sb("slot_token", [P, SLOT_TILES])
        no_token = sb("no_token", [P, SLOT_TILES])
        row = sb("row", [P, SLOT_TILES], U32)
        token = sb("token", [P, SLOT_TILES], U32)
        XS = sb("XS", [P, SLOT_TILES, ROW])
        XN = sb("XN", [P, 2, P])
        XT = sb("XT", [P, 2, P])
        W1K = sb("W1K", [P, 2, HID])
        HT2 = sb("HT2", [P, 2, HID])
        YS = sb("YS", [P, SLOT_TILES, P])
        banks = [stack.enter_context(nc.psum_tensor(f"bank{i}", [P, 512], F32)) for i in range(8)]
        tokens_dram = nc.dram_tensor("tokens_dram", (T * J, ROW), F32)
        d_scratch = nc.dram_tensor("d_scratch", (1, SK_SIZE), F32)
        v_scratch = nc.dram_tensor("v_scratch", (1, SK_SIZE), F16)

        def skewed(scratch, s0, s1):
            return bass.AP(scratch, (CH - 1) * CW + s0 * PITCH,
                           [[LANE_STRIDE, LANES], [PITCH, s1 - s0], [1, CW]])

        def rows_of(scratch, b, r0, r1):
            return bass.AP(scratch, b * CH * LANE_STRIDE + (CH - 1 + r0) * PITCH, [[PITCH, r1 - r0], [1, J]])

        def rows_of_all(scratch, r0, r1):
            return bass.AP(scratch, (CH - 1 + r0) * PITCH, [[PITCH, r1 - r0], [CH * LANE_STRIDE, T], [1, J]])

        x_in = [sem(f"x_in{t}") for t in range(T)]; w_in = sem("w_in"); wc_done = sem("wc_done"); wc_copied = sem("wc_copied")
        dk_done = sem("dk_done"); prod_done = sem("prod_done"); prod_old_done = sem("prod_old_done"); rstd_done = sem("rstd_done"); dv_done = sem("dv_done"); scored = sem("scored"); attn_in = sem("attn_in"); ctx_in = sem("ctx_in")
        moe_in = sem("moe_in"); gate_in = sem("gate_in"); out_done = sem("out_done")
        const_done = sem("const_done"); pool_step = sem("pool_step"); lanes_done = sem("lanes_done")
        dve_step = sem("dve_step");
        var_done = sem("var_done"); std_done = sem("std_done"); norm_done = sem("norm_done")
        tr_done = sem("tr_done"); tr_copied = sem("tr_copied")
        qkv_done = sem("qkv_done"); qkv_copied = sem("qkv_copied")
        xb_done = sem("xb_done"); split_done = sem("split_done"); exp_done = sem("exp_done")
        att_done = sem("att_done"); proj_done = sem("proj_done"); x1_done = sem("x1_done")
        m2_done = sem("m2_done"); sq_done = sem("sq_done"); dist_done = sem("dist_done")
        d2_done = sem("d2_done"); d_done = sem("d_done")
        prefill = sem("prefill"); d_out = sem("d_out"); dsk_in = [sem(f"dsk_in{n}") for n in range(len(DIST_PARTS))]
        low_done = sem("low_done"); scan_done = sem("scan_done"); mask_done = sem("mask_done")
        codes_done = [sem(f"codes_done{n}") for n in range(len(CODE_PARTS))]; codes_out = sem("codes_out"); blocks_in = sem("blocks_in"); ctxb_in = sem("ctxb_in"); ctxb_clear = sem("ctxb_clear")
        path_clear = sem("path_clear"); comp_done = sem("comp_done"); below_done = sem("below_done"); dia_known = sem("dia_known"); parts_ready = sem("parts_ready"); crossed_done = sem("crossed_done"); upto_done = sem("upto_done"); gwc_done = sem("gwc_done"); gwc_copied = sem("gwc_copied"); ctxg_done = sem("ctxg_done"); parts_done = sem("parts_done"); ctxg_copied = sem("ctxg_copied")
        picked0 = sem("picked0"); picked1 = sem("picked1")
        path_done = sem("path_done"); exp2_done = sem("exp2_done"); x2_done = sem("x2_done")
        lsh_done = sem("lsh_done"); lexp_done = sem("lexp_done")
        rw_done = sem("rw_done"); placed = sem("placed"); listed = sem("listed")
        hit_done = sem("hit_done"); expert_done = sem("expert_done")
        count_done = sem("count_done"); tokens_out = sem("tokens_out"); row_done = sem("row_done"); gathered = [sem(f"gathered{k}") for k in range(SLOT_TILES)]
        token_done = sem("token_done"); xt_done = sem("xt_done"); xt_copied = sem("xt_copied")
        hid_done = sem("hid_done"); hid_act = sem("hid_act"); w1_copied = sem("w1_copied"); xn_done = sem("xn_done"); xr_done = sem("xr_done")
        y_done = sem("y_done"); ys_done = sem("ys_done")

        block = stack.enter_context(nc.Block())
        x_v = x.rearrange("t (n p) d -> p (t n) d", p=P)
        out_v = out.rearrange("t (n p) d -> p (t n) d", p=P)
        SK = CW + 1

        @block.sync
        def _(sp):
            sp.dma_start(X[:, 0:TPB], x_v[:, 0:TPB]).then_inc(x_in[0], 16)
            sp.dma_start(wqkv[:], qkv_wt).then_inc(w_in, 16)
            sp.dma_start(X[:, TPB:], x_v[:, TPB:]).then_inc(x_in[1], 16)
            sp.dma_start(bqkv[:], qkv_b.partition_broadcast(P)).then_inc(attn_in, 16)
            sp.dma_start(wo[:], out_wt).then_inc(attn_in, 16)
            sp.dma_start(bo[:], out_b.partition_broadcast(P)).then_inc(attn_in, 16)
            sp.dma_start(ctxT[:, :, PAD:], ctx_t.rearrange("d (b r) -> d b r", b=T)).then_inc(ctx_in, 16)
            sp.dma_start(ctxr[:], ctx_rows.rearrange("t r d -> r t d")).then_inc(ctx_in, 16)
            sp.wait_ge(ctxb_clear, 1)
            for b in range(T):
                sp.dma_start(ctxb[32 * b + 1:32 * b + NB, :, 0:P], ctx_rows[b, KB - PAD:].rearrange("(g r) d -> g r d", r=KB)
                             ).then_inc(ctxb_in, 16)
                sp.dma_start(ctxb[32 * b:32 * b + 1, PAD:, 0:P], ctx_rows[b:b + 1, 0:KB - PAD]).then_inc(ctxb_in, 16)
            sp.dma_start(gw[:], gate_w).then_inc(gate_in, 16)
            sp.dma_start(gb[:], gate_b.partition_broadcast(P)).then_inc(gate_in, 16)
            sp.dma_start(B1[:].rearrange("p e c -> p (e c)"), b1_t).then_inc(moe_in, 16)
            sp.dma_start(B2[:].rearrange("p e d -> p (e d)"),
                         b2.rearrange("e d -> (e d)").partition_broadcast(P)).then_inc(moe_in, 16)
            sp.wait_ge(lanes_done, 1)
            for r0 in (1 - CH, ROWS):
                sp.dma_start(rows_of_all(d_scratch, r0, r0 + CH - 1), big_rows[:]).then_inc(prefill, 16)
            sp.dma_start(W1[:], w1.rearrange("e d h -> d e h")).then_inc(moe_in, 16)
            sp.dma_start(W2[:], w2.rearrange("e (c p) d -> p e c d", p=P)).then_inc(moe_in, 16)
            sp.wait_ge(prefill, 32)
            for b in range(T):
                sp.wait_ge(d_done, b + 1)
                sp.dma_start(rows_of(d_scratch, b, 0, ROWS), D[:, b, :]).then_inc(d_out, 16)
            sp.wait_ge(d_out, 32)
            for n, (s0, s1) in enumerate(DIST_PARTS):
                sp.dma_start(Dsk[:, s0:s1, 1:], skewed(d_scratch, s0, s1)).then_inc(dsk_in[n], 16)
            sp.dma_start(rows_of_all(v_scratch, -PAD, 0), zero_row[:]).then_inc(codes_out, 16)
            sp.wait_ge(codes_out, 16)
            for n, (s0, s1) in enumerate(CODE_PARTS):
                sp.wait_ge(codes_done[n], 1)
                sp.dma_start(skewed(v_scratch, s0, s1), V[:, s0:s1]).then_inc(codes_out, 16)
                sp.wait_ge(codes_out, 16 + 16 * (n + 1))
                g0, g1 = (NB if s == STEPS else max(s - CH + 1 + PAD, 0) // KB for s in (s0, s1))
                for b in range(T):
                    sp.dma_start(VB[32 * b + g0:32 * b + g1],
                                 rows_of(v_scratch, b, KB * g0 - PAD, KB * g1 - PAD).rearrange(
                                     "(g r) j -> g r j", r=KB)).then_inc(blocks_in, 16)
            tokens_v = tokens_dram.ap().rearrange("(n p) f -> p n f", p=P)
            for b in range(T):
                sp.wait_ge(x2_done, NT // T // 2 * (b + 1))
                sp.dma_start(tokens_v[:, b * TPB:(b + 1) * TPB, 0:P],
                             X2[:, b * TPB:(b + 1) * TPB, :]).then_inc(tokens_out, 16)
            sp.wait_ge(rw_done, 1)
            sp.dma_start(tokens_v[:, :, P:ROW], norm_gate[:]).then_inc(tokens_out, 16)

        def follow_path(eng, copy, b, done):
            eng.wait_ge(comp_done, 1)
            eng.wait_ge(const_done, 2)
            col = J
            for g in range(NB - 1, -1, -1):
                lane = 32 * b + g
                copy(picked[32 * b:32 * b + NB, g:g + 1],
                     codes[32 * b:32 * b + NB, bass.ds(col, 1)]).then_inc(done, 1)
                if g:
                    exit_code = eng.value_load(block_table[lane:lane + 1, bass.ds(col, 1)])
                    col = nc.s_assert_within(exit_code // 2, 0, J, skip_runtime_bounds_check_because=
                                             "a code is twice a column of the row and two, or one less")

        def expert_of(eng, k):
            return nc.s_assert_within(eng.value_load(expert[0:1, k:k + 1]), 0, NE - 1,
                                      skip_runtime_bounds_check_because="the last expert is the largest number")

        @block.gpsimd
        def _(pool):
            steps = [0]

            def step(i):
                steps[0] += 1
                i.then_inc(pool_step, 1)
                pool.wait_ge(pool_step, steps[0])

            step(nc.gpsimd.memset(ident[:], 0.0))
            step(nc.gpsimd.affine_select(out=ident[:], in_=ident[:], pattern=[[-1, P]], compare_op=ALU.not_equal,
                                         fill=1.0, base=0, channel_multiplier=1))
            step(nc.gpsimd.memset(center[:], -1.0 / P))
            step(nc.gpsimd.affine_select(out=center[:], in_=center[:], pattern=[[-1, P]], compare_op=ALU.not_equal,
                                         fill=1.0 - 1.0 / P, base=0, channel_multiplier=1))
            step(nc.gpsimd.memset(ones[:], 1.0))
            step(nc.gpsimd.memset(eps_col[:], EPS))
            pool.sem_inc(const_done, 1)
            step(nc.gpsimd.memset(ctxb[:], 0.0))
            step(nc.gpsimd.memset(ctxT[:, :, 0:PAD], 0.0))
            step(nc.gpsimd.tensor_copy(carry[:, 0:P], ident[:]))
            pool.sem_inc(ctxb_clear, 1)
            for t in range(T):
                pool.wait_ge(x_in[t], 16)
            pool.wait_ge(attn_in, 48)
            step(nc.gpsimd.tensor_tensor(XB[:], X[:], bo[:].unsqueeze(1).to_broadcast([P, NT, P]), ALU.add))
            pool.sem_inc(xb_done, 1)
            for i in range(TPB):
                pool.wait_ge(qkv_copied, 2 * (i + 1))
                step(nc.gpsimd.tensor_tensor(prod[:, 0, i, :], QKV[:, i, 0:P], QKV[:, i, P:2 * P], ALU.mult))
                pool.sem_inc(prod_old_done, 1)
            step(nc.gpsimd.tensor_tensor(dv[:], QKV[:, TPB:, 2 * P:], QKV[:, 0:TPB, 2 * P:], ALU.subtract))
            pool.sem_inc(dv_done, 1)
            step(nc.gpsimd.memset(Dsk[:, :, 0:1], 0.0))
            step(nc.gpsimd.memset(R[:, 0, :], BIG))
            for b in range(T):
                step(nc.gpsimd.affine_select(out=Dsk[:, :, 0:1], in_=Dsk[:, :, 0:1], pattern=[[0, STEPS], [0, 1]],
                                             compare_op=ALU.not_equal, fill=BIG, base=-(CH * (b + 1) - 1),
                                             channel_multiplier=1))
                step(nc.gpsimd.affine_select(out=R[:, 0, 0:1], in_=R[:, 0, 0:1], pattern=[[0, 1]],
                                             compare_op=ALU.not_equal, fill=0.0, base=-(CH * (b + 1) - 1),
                                             channel_multiplier=1))
            step(nc.gpsimd.memset(big_rows[:], BIG))
            step(nc.gpsimd.memset(zero_row[:], 0.0))
            pool.sem_inc(lanes_done, 1)
            step(nc.gpsimd.iota(col2[:], pattern=[[2, CW]], base=2 + 2 * CW * (CH - 1), channel_multiplier=-2 * CW,
                                allow_small_or_imprecise_dtypes=True))
            step(nc.gpsimd.memset(next_batch[:], float(2 * J)))
            step(nc.gpsimd.affine_select(out=next_batch[:], in_=next_batch[:], pattern=[[0, CW]],
                                         compare_op=ALU.is_ge, fill=0.0, base=-CH, channel_multiplier=1))
            step(nc.gpsimd.tensor_tensor(col2[:], col2[:], next_batch[:], ALU.add))
            step(nc.gpsimd.iota(codes[:], pattern=[[2, J + 1]], base=0, channel_multiplier=0,
                                allow_small_or_imprecise_dtypes=True))
            step(nc.gpsimd.iota(odd_codes[:], pattern=[[2, J]], base=1, channel_multiplier=0,
                                allow_small_or_imprecise_dtypes=True))
            step(nc.gpsimd.memset(block_diag[:], 0.0))
            for b in range(T):
                step(nc.gpsimd.affine_select(out=block_diag[32 * b:32 * b + 32], in_=block_diag[32 * b:32 * b + 32],
                                             pattern=[[-1, NB]], compare_op=ALU.not_equal, fill=1.0, base=0,
                                             channel_multiplier=1))
            step(nc.gpsimd.iota(rev_e[:], pattern=[[-1, NE]], base=NE, channel_multiplier=0,
                                allow_small_or_imprecise_dtypes=True))
            step(nc.gpsimd.iota(tile_no[:], pattern=[[P, NE]], base=0, channel_multiplier=0,
                                allow_small_or_imprecise_dtypes=True))
            step(nc.gpsimd.iota(slot_tile[:], pattern=[[1, SLOT_TILES]], base=0, channel_multiplier=0,
                                allow_small_or_imprecise_dtypes=True))
            step(nc.gpsimd.iota(token_tile[:], pattern=[[P, NT]], base=0, channel_multiplier=0,
                                allow_small_or_imprecise_dtypes=True))
            step(nc.gpsimd.iota(part_no[:], pattern=[[0, 1]], base=1, channel_multiplier=1,
                                allow_small_or_imprecise_dtypes=True))
            step(nc.gpsimd.iota(slot_no_f[:], pattern=[[1, P]], base=0, channel_multiplier=0,
                                allow_small_or_imprecise_dtypes=True))
            step(nc.gpsimd.tensor_copy(slot_no[:], slot_no_f[:]))
            step(nc.gpsimd.memset(ones_h[:], 1.0))
            step(nc.gpsimd.affine_select(out=before[:], in_=ones_h[:], pattern=[[1, P]],
                                         compare_op=ALU.is_gt, fill=0.0, base=0, channel_multiplier=-1))
            pool.sem_inc(const_done, 1)
            pool.wait_ge(ctxb_in, 64)
            pool.wait_ge(ctxg_copied, 2)
            for part, rest in enumerate((ctxb, ctxb_rest, ctxb_rest)):
                step(nc.gpsimd.tensor_copy(ctxb_part[:, :, part, :], rest[:]))
                if part < 2:
                    step(nc.gpsimd.tensor_tensor(ctxb_rest[:], rest[:], ctxb_part[:, :, part, :], ALU.subtract))
            pool.sem_inc(parts_done, 1)
            pool.wait_ge(x1_done, 2)
            for t in (VB, picked):
                step(nc.gpsimd.memset(t[:], 0.0))
            pool.sem_inc(path_clear, 1)
            for n, (s0, s1) in enumerate(CODE_PARTS[:-1]):
                pool.wait_ge(mask_done, 2 * s1 + (s1 < STEPS))
                cols = col2[:].unsqueeze(1).to_broadcast([LANES, s1 - s0, CW])
                step(nc.gpsimd.tensor_tensor(V[:, s0:s1], cols, dg[:, s0:s1], ALU.subtract))
                step(nc.gpsimd.tensor_tensor(V[:, s0:s1], V[:, s0:s1], notleft[:, s0:s1], ALU.mult))
                pool.sem_inc(codes_done[n], 1)
            follow_path(pool, nc.gpsimd.tensor_copy, 1, picked1)
            pool.wait_ge(tokens_out, 16 * (T + 1))
            pool.wait_ge(row_done, 1)

            def fetch(k):
                nc.gpsimd.indirect_dma_start(
                    out=XS[:, k, :], out_offset=None, in_=tokens_dram.ap(),
                    in_offset=bass.IndirectOffsetOnAxis(row[:, k:k + 1], 0), bounds_check=T * J - 1,
                    oob_is_err=False).then_inc(gathered[k], 16)

            for k in range(AHEAD):
                fetch(k)
            pool.wait_ge(token_done, 1)
            for k in range(SLOT_TILES):
                if k + AHEAD < SLOT_TILES:
                    fetch(k + AHEAD)
                pool.wait_ge(ys_done, k + 1)
                nc.gpsimd.indirect_dma_start(
                    out=out.rearrange("t j d -> (t j) d"),
                    out_offset=bass.IndirectOffsetOnAxis(token[:, k:k + 1], 0),
                    in_=YS[:, k, :], in_offset=None, bounds_check=T * J - 1,
                    oob_is_err=False).then_inc(out_done, 16)
            pool.wait_ge(out_done, 16 * SLOT_TILES)

        @block.vector
        def _(dve):
            steps = [0]

            def step(i):
                steps[0] += 1
                i.then_inc(dve_step, 1)
                dve.wait_ge(dve_step, steps[0])

            def statistics(k, src, tiles):
                for n in tiles:
                    i = nc.vector.bn_stats(stats[:, k, n, :], src[:, n, :])
                step(i)
                for n in tiles:
                    i = nc.vector.bn_aggr(mean_var[:, k, n, :], stats[:, k, n, :])
                i.then_inc(var_done, 1)

            def batch(t):
                return range(t * TPB, (t + 1) * TPB)

            for t in range(T):
                dve.wait_ge(x_in[t], 16)
                for n in batch(t):
                    i = nc.vector.bn_stats(stats[:, 0, n, :], X[:, n, :])
            step(i)
            for n in range(NT):
                i = nc.vector.bn_aggr(mean_var[:, 0, n, :], stats[:, 0, n, :])
            i.then_inc(var_done, 1)
            dve.wait_ge(std_done, 1)
            step(nc.vector.reciprocal(rstd[:, 0, :], std[:, 0, :]))
            dve.wait_ge(attn_in, 48)
            q, k, v = (QKV[:, :, i * P:(i + 1) * P] for i in range(3))

            def reduce_pair(i):
                dve.wait_ge(prod_done, i + 1)
                dve.wait_ge(prod_old_done, i + 1)
                nc.vector.tensor_reduce(score[:, :, i * HEADS:(i + 1) * HEADS],
                                        prod[:, :, i, :].rearrange("p t (h d) -> p t h d", d=DH),
                                        AX_X, ALU.add).then_inc(scored, 1)

            for i in range(TPB + 1):
                if i < TPB:
                    for m, n in enumerate((i, i + TPB)):
                        dve.wait_ge(qkv_done, 2 * i + m + 1)
                        nc.vector.scalar_tensor_tensor(out=QKV[:, n, :], in0=banks[(2 * i + m + 2) % 8][:, 0:3 * P],
                                                       scalar=rstd[:, 0, n:n + 1], in1=bqkv[:], op0=ALU.mult,
                                                       op1=ALU.add).then_inc(qkv_copied, 1)
                        if m == 0 and i:
                            dve.wait_ge(qkv_copied, 2 * i)
                            nc.vector.tensor_tensor(dk[:, i - 1, :], k[:, i - 1 + TPB, :], k[:, i - 1, :],
                                                    ALU.subtract).then_inc(dk_done, 1)
                else:
                    dve.wait_ge(qkv_copied, 2 * i)
                    nc.vector.tensor_tensor(dk[:, i - 1, :], k[:, i - 1 + TPB, :], k[:, i - 1, :],
                                            ALU.subtract).then_inc(dk_done, 1)
                if i:
                    dve.wait_ge(dk_done, i)
                    nc.vector.tensor_tensor(prod[:, 1, i - 1, :], q[:, i - 1 + TPB, :], dk[:, i - 1, :],
                                            ALU.mult).then_inc(prod_done, 1)
                    if i >= 2:
                        reduce_pair(i - 2)
            reduce_pair(TPB - 1)
            dve.wait_ge(scored, TPB)
            t0, t1 = slice(0, TPB), slice(TPB, NT)
            masked = nc.vector.tensor_scalar(dif[:], score[:, 0], -(DH ** -0.5), MASKED, ALU.mult, ALU.add)
            steps[0] += 1
            masked.then_inc(dve_step, 1)
            nc.vector.tensor_scalar(dif_hi[:, 1], score[:, 1], DH ** -0.5, 0.0, ALU.mult, ALU.max)
            nc.vector.tensor_scalar(dif_lo[:, 1], score[:, 1], DH ** -0.5, 0.0, ALU.mult, ALU.min)
            dve.wait_ge(dve_step, steps[0])
            nc.vector.tensor_scalar(dif_hi[:, 0], dif[:], 0.0, None, ALU.max)
            nc.vector.tensor_scalar(dif_lo[:, 0], dif[:], 0.0, None, ALU.min).then_inc(split_done, 1)
            dve.wait_ge(exp_done, 2)
            step(nc.vector.tensor_tensor(exp_sum[:], exp_old[:], exp_new[:], ALU.add))
            step(nc.vector.reciprocal(exp_rec[:], exp_sum[:]))
            step(nc.vector.tensor_tensor(prob[:], exp_new[:], exp_rec[:], ALU.mult))
            dve.wait_ge(dv_done, 1)
            for t in range(T):
                i = nc.vector.tensor_tensor(
                    pdv[:, t].rearrange("p n (h d) -> p (n h) d", d=DH),
                    prob[:, t].unsqueeze(2).to_broadcast([P, TPB * HEADS, DH]),
                    dv[:].rearrange("p n (h d) -> p (n h) d", d=DH), ALU.mult)
            step(i)
            for t in range(T):
                nc.vector.tensor_tensor(att[:, t * TPB:(t + 1) * TPB, :], pdv[:, t], v[:, t0, :],
                                        ALU.add).then_inc(att_done, 1)
            dve.wait_ge(ctx_in, 32)
            nc.vector.tensor_scalar(ctxTm2[:].rearrange("d (b r) -> d b r", b=T), ctxT[:, :, PAD:], -2.0, None, ALU.mult).then_inc(m2_done, 1)
            step(nc.vector.tensor_tensor(ctxsq[:], ctxr[:], ctxr[:], ALU.mult))
            nc.vector.tensor_reduce(aa[:], ctxsq[:], AX_X, ALU.add)
            dve.wait_ge(xb_done, 1)
            for t in range(T):
                dve.wait_ge(proj_done, t + 1)
                nc.vector.tensor_tensor(X1[:, t * TPB:(t + 1) * TPB, :],
                                        banks[4 + t][:].rearrange("p (n d) -> p n d", d=P),
                                        XB[:, t * TPB:(t + 1) * TPB, :], ALU.add).then_inc(x1_done, 1)
                dve.wait_ge(x1_done, t + 1)
                if t == 0:
                    statistics(1, X1, batch(t))
            for t in range(T):
                if t:
                    statistics(1, X1, batch(t))
                dve.wait_ge(std_done, 2 + t)
                nc.vector.reciprocal(rstd[:, 1, t * TPB:(t + 1) * TPB],
                                     std[:, 1, t * TPB:(t + 1) * TPB]).then_inc(rstd_done, 1)
                dve.wait_ge(rstd_done, t + 1)
                for n in batch(t):
                    i = nc.vector.tensor_scalar(S[:, n, :], X1[:, n, :], mean_var[:, 1, n, 0:1],
                                                rstd[:, 1, n:n + 1], ALU.subtract, ALU.mult)
                i.then_inc(norm_done, 1)
            for b in range(T):
                dve.wait_ge(dist_done, b + 1)
                nc.vector.tensor_scalar(D[:, b, :], banks[1 + b][0:ROWS, :], aa[:, b:b + 1], 0.0, ALU.add,
                                        ALU.max).then_inc(d2_done, 1)

            shift = list(range(1, LANES)) + [LANES - 1]
            dve.wait_ge(lanes_done, 1)
            for s in range(STEPS):
                if s in [p[0] for p in DIST_PARTS]:
                    dve.wait_ge(dsk_in[[p[0] for p in DIST_PARTS].index(s)], 16)
                if s:
                    dve.wait_ge(scan_done, s)
                nc.vector.tensor_tensor(M[:, s, 1:SK], R[:, s, 1:SK], R[:, s, 0:CW], ALU.min).then_inc(low_done, 1)
                nc.vector.stream_shuffle(M[:, s, 0:1], R[:, s, CW:SK], shift).then_inc(low_done, 1)
                nc.vector.tensor_tensor(dg[:, s, :], R[:, s, 0:CW], R[:, s, 1:SK], ALU.is_le).then_inc(mask_done, 1)
                dve.wait_ge(low_done, 2 * s + 2)
                nc.vector.tensor_tensor_scan(R[:, s + 1, :], M[:, s, :], Dsk[:, s, :], BIG, ALU.min,
                                             ALU.add).then_inc(scan_done, 1)
                if s:
                    nc.vector.tensor_tensor(notleft[:, s - 1, :], R[:, s, 0:CW], M[:, s - 1, 1:SK],
                                            ALU.is_ge).then_inc(mask_done, 1)
            s0, s1 = CODE_PARTS[-1]
            dve.wait_ge(const_done, 2)
            dve.wait_ge(mask_done, 2 * STEPS - 2)
            nc.vector.tensor_tensor(V[:, s0:s1], col2[:].unsqueeze(1).to_broadcast([LANES, s1 - s0, CW]),
                                    dg[:, s0:s1], ALU.subtract).then_inc(mask_done, 1)
            dve.wait_ge(scan_done, STEPS)
            nc.vector.tensor_tensor(notleft[:, STEPS - 1, :], R[:, STEPS, 0:CW], M[:, STEPS - 1, 1:SK],
                                    ALU.is_ge).then_inc(mask_done, 1)
            dve.wait_ge(mask_done, 2 * STEPS + 1)
            nc.vector.tensor_tensor(V[:, s0:s1], V[:, s0:s1], notleft[:, s0:s1], ALU.mult).then_inc(codes_done[-1], 1)

            def running(dst, a, b_):
                return nc.vector.tensor_tensor_scan(dst, a, b_, 0.0, ALU.max, ALU.max)

            dve.wait_ge(path_clear, 1)
            nc.vector.memset(diag_part[:, 0:1], 0.0)
            nc.vector.memset(block_table[:, 0:1], 0)
            dve.wait_ge(blocks_in, 32 * len(CODE_PARTS))

            def leaves_up(r):
                nc.vector.tensor_tensor(exit_up[:, r - 1], VB[:, r], codes[0:BP, 1:], ALU.is_equal)

            def leaves_diagonally(r):
                nc.vector.tensor_tensor(exit_dia[:, r - 1], VB[:, r], odd_codes[:],
                                        ALU.is_equal).then_inc(dia_known, 1)

            leaves_up(1)
            running(code[:, 0], VB[:, 0], VB[:, 0]).then_inc(below_done, 1)
            leaves_diagonally(1)
            below = code[:, 0]
            for r in range(1, KB):
                dve.wait_ge(below_done, r)
                nc.vector.tensor_tensor(up_part[:], exit_up[:, r - 1], below, ALU.mult)
                dve.wait_ge(dia_known, r)
                nc.vector.tensor_tensor(diag_part[:, 1:], exit_dia[:, r - 1, 1:], below[:, 0:J - 1],
                                        ALU.mult).then_inc(parts_ready, 1)
                if r < KB - 1:
                    leaves_up(r + 1)
                    dve.wait_ge(parts_ready, r)
                    running(comp[:, r - 1], up_part[:], diag_part[:]).then_inc(below_done, 1)
                    leaves_diagonally(r + 1)
                    below = comp[:, r - 1]
                else:
                    dve.wait_ge(parts_ready, r)
                    running(block_table[:, 1:], up_part[:], diag_part[:]).then_inc(comp_done, 1)
            for r in range(1, KB):
                i = running(code[:, r], VB[:, r], VB[:, r])
            step(i)
            nc.vector.tensor_copy(jump[:, :, 0:1], code[:, :, 0:1])
            step(nc.vector.tensor_tensor(jump[:, :, 1:], code[:, :, 1:], code[:, :, 0:J - 1], ALU.subtract))
            dve.wait_ge(picked0, NB)
            dve.wait_ge(picked1, NB)
            step(nc.vector.scalar_tensor_tensor(out=diag[:], in0=picked[:], scalar=1.0, in1=block_diag[:],
                                                op0=ALU.mult, op1=ALU.mult, accum_out=entry[:, 0:1]))
            def cross(m):
                r = KB - 1 - m
                nc.vector.scalar_tensor_tensor(out=crossed[:, r], in0=codes[0:BP, 1:], scalar=entry[:, m:m + 1],
                                               in1=jump[:, r], op0=ALU.is_le, op1=ALU.mult,
                                               accum_out=entry[:, m + 1:m + 2]).then_inc(crossed_done, 1)

            cross(0)
            for m in range(KB):
                r = KB - 1 - m
                nc.vector.tensor_scalar(upto[:, r], codes[0:BP, 1:], entry[:, m:m + 1], None,
                                        ALU.is_le).then_inc(upto_done, 1)
                dve.wait_ge(crossed_done, m + 1)
                if m + 1 < KB:
                    cross(m + 1)
                dve.wait_ge(upto_done, m + 1)
                nc.vector.scalar_tensor_tensor(out=onpath[:, r], in0=codes[0:BP, 1:], scalar=entry[:, m + 1:m + 2],
                                               in1=upto[:, r], op0=ALU.is_ge, op1=ALU.mult).then_inc(path_done, 1)
            pair_of = [banks[2 + n][:, 0:2 * (P + NE)].rearrange("p (n f) -> p n f", f=P + NE) for n in range(NT // 2)]
            for b in range(T):
                dve.wait_ge(exp2_done, b + 1)
                if b:
                    for n in batch(0):
                        nc.vector.bn_aggr(mean_var[:, 2, n, :], stats[:, 2, n, :])
                for n in batch(b):
                    i = nc.vector.bn_stats(stats[:, 2, n, :], pair_of[n // 2][:, n % 2, 0:P])
                step(i)
            for n in batch(1):
                i = nc.vector.bn_aggr(mean_var[:, 2, n, :], stats[:, 2, n, :])
            i.then_inc(var_done, 1)
            dve.wait_ge(std_done, 4)
            step(nc.vector.reciprocal(rstd[:, 2, :], std[:, 2, :]))

            dve.wait_ge(const_done, 2)
            dve.wait_ge(gate_in, 32)

            def spread(col):
                return col.unsqueeze(2).to_broadcast([P, TPB, NE])

            def by_batch(op):
                for t in range(T):
                    steps[0] += 1
                    op(slice(t * TPB, (t + 1) * TPB)).then_inc(dve_step, 1)
                    dve.wait_ge(dve_step, steps[0] - 1)

            rank = banks[6][:, NT * NE:2 * NT * NE].rearrange("p (n e) -> p n e", e=NE)
            rev_b = rev_e[:].unsqueeze(1).to_broadcast([P, TPB, NE])
            for n in range(0, NT, 2):
                i = nc.vector.tensor_tensor(G[:, n:n + 2, :], pair_of[n // 2][:, :, P:],
                                            rstd[:, 2, n:n + 2].unsqueeze(2).to_broadcast([P, 2, NE]), ALU.mult)
            step(i)
            by_batch(lambda b: nc.vector.tensor_tensor(logit[:, b], G[:, b],
                                                       gb[:].unsqueeze(1).to_broadcast([P, TPB, NE]), ALU.add))
            by_batch(lambda b: nc.vector.tensor_reduce(lmax[:, b], logit[:, b], AX_X, ALU.max))
            by_batch(lambda b: nc.vector.tensor_tensor(lsh[:, b], logit[:, b], spread(lmax[:, b]), ALU.subtract))
            dve.wait_ge(dve_step, steps[0])
            dve.sem_inc(lsh_done, 1)
            dve.wait_ge(lexp_done, 1)
            by_batch(lambda b: nc.vector.tensor_reduce(lsum[:, b], lexp[:, b], AX_X, ALU.add))
            by_batch(lambda b: nc.vector.reciprocal(lrec[:, b], lsum[:, b]))
            by_batch(lambda b: nc.vector.tensor_tensor(gs[:, b], lexp[:, b], spread(lrec[:, b]), ALU.mult))
            for r, left in ((0, gs), (1, gs2)):
                by_batch(lambda b: nc.vector.tensor_reduce(top[:, r, b], left[:, b], AX_X, ALU.max))
                by_batch(lambda b: nc.vector.tensor_tensor(hit[:, r, b], left[:, b], spread(top[:, r, b]), ALU.is_equal))
                if r:
                    steps[0] += 1
                    nc.vector.tensor_scalar(absent[:], top[:, 1], 0.0, float(NE), ALU.is_le, ALU.mult).then_inc(dve_step, 1)
                    dve.wait_ge(dve_step, steps[0] - 1)
                by_batch(lambda b: nc.vector.tensor_tensor(rev[:, r, b], hit[:, r, b], rev_b, ALU.mult))
                by_batch(lambda b: nc.vector.tensor_reduce(first[:, r, b], rev[:, r, b], AX_X, ALU.max))
                if r == 0:
                    by_batch(lambda b: nc.vector.tensor_tensor(taken[:, b], rev_b, spread(first[:, 0, b]), ALU.is_equal))
                    by_batch(lambda b: nc.vector.scalar_tensor_tensor(
                        out=gs2[:, b], in0=taken[:, b], scalar=-2.0, in1=gs[:, b], op0=ALU.mult, op1=ALU.add))
            dve.wait_ge(dve_step, steps[0])
            step(nc.vector.tensor_tensor(absent[:], absent[:], first[:, 1], ALU.add))
            step(nc.vector.tensor_tensor(chosen[:], absent[:], first[:, 0], ALU.min))
            nc.vector.tensor_tensor(onehot[:], rev_e[:].unsqueeze(1).to_broadcast([P, NT, NE]),
                                    chosen[:].unsqueeze(2).to_broadcast([P, NT, NE]), ALU.is_equal).then_inc(hit_done, 1)
            dve.wait_ge(hit_done, 1)
            def count(i):
                steps[0] += 1
                i.then_inc(dve_step, 1)
                return steps[0]

            def await_step(n):
                dve.wait_ge(dve_step, n)

            weighted = count(nc.vector.tensor_tensor(wsel[:], onehot[:], gs[:], ALU.mult))
            first_end = count(nc.vector.memset(ends[:, 0:1], 0.0))
            dve.wait_ge(count_done, 1)
            ranked = count(nc.vector.tensor_tensor(rank_sel[:], rank, onehot[:], ALU.mult))
            await_step(weighted)
            summed = count(nc.vector.tensor_reduce(wgate[:], wsel[:], AX_X, ALU.add))
            dve.wait_ge(count_done, 2)
            compared = count(nc.vector.tensor_tensor(tiles_gt[:], banks[7][:, 0:NE].unsqueeze(2).to_broadcast([P, NE, NE]),
                                                     tile_no[:].unsqueeze(1).to_broadcast([P, NE, NE]), ALU.is_gt))
            await_step(ranked)
            ranked = count(nc.vector.tensor_reduce(rank_f[:], rank_sel[:], AX_X, ALU.add))
            await_step(summed)
            scaled = count(nc.vector.tensor_tensor(norm_gate[:, :, 0], rstd[:, 2, :], wgate[:], ALU.mult))
            await_step(compared)
            tiled = count(nc.vector.tensor_reduce(tiles_of[:], tiles_gt[:], AX_X, ALU.add))
            await_step(ranked)
            reached_done = count(nc.vector.tensor_tensor(
                reached[:], rank_f[:].unsqueeze(2).to_broadcast([P, NT, NE - 1]),
                tile_no[:, 1:].unsqueeze(1).to_broadcast([P, NT, NE - 1]), ALU.is_ge))
            await_step(scaled)
            shifted = count(nc.vector.scalar_tensor_tensor(out=norm_gate[:, :, 1], in0=mean_var[:, 2, :, 0],
                                                           scalar=-1.0, in1=norm_gate[:, :, 0], op0=ALU.mult,
                                                           op1=ALU.mult))
            await_step(tiled)
            ended_done = count(nc.vector.tensor_tensor_scan(ends[:, 1:], ones[:, 0:NE], tiles_of[:], 0.0,
                                                            ALU.mult, ALU.add))
            await_step(reached_done)
            filled = count(nc.vector.tensor_reduce(full_tiles[:], reached[:], AX_X, ALU.add))
            await_step(shifted)
            dve.sem_inc(rw_done, 1)
            await_step(ended_done)
            based = count(nc.vector.tensor_tensor(base_sel[:], ends[:, 0:NE].unsqueeze(1).to_broadcast([P, NT, NE]),
                                                  onehot[:], ALU.mult))
            await_step(filled)
            within_done = count(nc.vector.scalar_tensor_tensor(out=within[:], in0=full_tiles[:], scalar=-float(P),
                                                               in1=rank_f[:], op0=ALU.mult, op1=ALU.add))
            await_step(based)
            based = count(nc.vector.tensor_reduce(base_f[:], base_sel[:], AX_X, ALU.add))
            await_step(within_done)

            def mark_place(n):
                nc.vector.tensor_scalar(at_slot[:, n, :], slot_no[:], within[:, n:n + 1], None,
                                        ALU.is_equal).then_inc(placed, 1)

            mark_place(0)
            await_step(based)
            tile_known = count(nc.vector.tensor_tensor(tile_f[:], base_f[:], full_tiles[:], ALU.add))
            mark_place(1)
            await_step(tile_known)
            tile_known = count(nc.vector.tensor_tensor(in_tile[:], tile_f[:].unsqueeze(2).to_broadcast([P, NT, SLOT_TILES]),
                                                       slot_tile[:].unsqueeze(1).to_broadcast([P, NT, SLOT_TILES]),
                                                       ALU.is_equal))
            mark_place(2)
            await_step(tile_known)
            nc.vector.tensor_scalar(number[:, :, :, 1], in_tile[:], part_no[:, 0:1], None, ALU.mult)
            nc.vector.tensor_tensor(number[:, :, :, 0], in_tile[:],
                                    token_tile[:].unsqueeze(2).to_broadcast([P, NT, SLOT_TILES]),
                                    ALU.mult).then_inc(placed, 1)
            for n in range(3, NT):
                mark_place(n)
            step(nc.vector.tensor_tensor(ended[:], ends[:, 1:].unsqueeze(1).to_broadcast([P, SLOT_TILES, NE]),
                                         slot_tile[:].unsqueeze(2).to_broadcast([P, SLOT_TILES, NE]), ALU.is_le))
            step(nc.vector.tensor_reduce(expert_f[:], ended[:], AX_X, ALU.add))
            nc.vector.tensor_scalar(expert[:], expert_f[:], float(NE - 1), None, ALU.min).then_inc(expert_done, 1)
            dve.wait_ge(listed, 1)
            step(nc.vector.tensor_reduce(slot_token[:], banks[1][:, 0:2 * SLOT_TILES].rearrange("p (k q) -> p k q", q=2),
                                         AX_X, ALU.add))
            nc.vector.tensor_scalar(row[:], slot_token[:], -1.0, 0.0, ALU.add, ALU.max).then_inc(row_done, 1)
            step(nc.vector.tensor_scalar(no_token[:], slot_token[:], 0.0, float(NO_TOKEN), ALU.is_equal, ALU.mult))
            nc.vector.scalar_tensor_tensor(out=token[:], in0=no_token[:], scalar=-1.0, in1=slot_token[:],
                                           op0=ALU.add, op1=ALU.add).then_inc(token_done, 1)
            dve.wait_ge(expert_done, 1)
            dve.wait_ge(moe_in, 64)
            for k in range(SLOT_TILES + 1):
                if k < SLOT_TILES:
                    e = expert_of(dve, k)
                    dve.wait_ge(gathered[k], 16)
                    nc.vector.tensor_tensor(YS[:, k, :], XS[:, k, 0:P], B2[:, bass.ds(e, 1), :].squeeze(1),
                                            ALU.add).then_inc(xr_done, 1)
                    dve.wait_ge(hid_done, k + 1)
                    if k >= 2:
                        dve.wait_ge(y_done, k - 1)
                    for c in range(HC):
                        i = nc.vector.tensor_scalar(HT2[:, k % 2, c * P:(c + 1) * P],
                                                    banks[2 + k % 2][:, c * P:(c + 1) * P],
                                                    B1[:, bass.ds(e, 1), c:c + 1].squeeze(1), 0.0, ALU.add, ALU.max)
                    i.then_inc(hid_act, 1)
                if k:
                    dve.wait_ge(y_done, k)
                    dve.wait_ge(xr_done, k)
                    nc.vector.tensor_tensor(YS[:, k - 1, :], banks[6 + (k - 1) % 2][:, 0:P], YS[:, k - 1, :],
                                            ALU.add).then_inc(ys_done, 1)

        @block.scalar
        def _(act):
            act.wait_ge(const_done, 1)
            nc.scalar.activation(root_of_eps[:], eps_col[:], ACT.Sqrt)

            def root(k, tiles):
                nc.scalar.activation(std[:, k, tiles], mean_var[:, k, tiles, 1], ACT.Sqrt,
                                     bias=eps_col[:]).then_inc(std_done, 1)

            def copy_t(dst, first_bank, count):
                for t in range(T):
                    act.wait_ge(tr_done, count + t + 1)
                    nc.scalar.copy(dst[:, t * J:(t + 1) * J], banks[first_bank + t][:]).then_inc(tr_copied, 1)

            act.wait_ge(wc_done, 1)
            nc.scalar.copy(wc[:], banks[7][:, 0:3 * P]).then_inc(wc_copied, 1)
            copy_t(XTT, 0, 0)
            act.wait_ge(var_done, 1)
            root(0, slice(0, NT))
            act.wait_ge(split_done, 1)
            nc.scalar.activation(exp_old[:], dif_hi[:], ACT.Exp, scale=-1.0).then_inc(exp_done, 1)
            nc.scalar.activation(exp_new[:], dif_lo[:], ACT.Exp).then_inc(exp_done, 1)
            copy_t(attT, 2, 2)
            for t in range(T):
                act.wait_ge(var_done, 2 + t)
                root(1, slice(t * TPB, (t + 1) * TPB))
            for t in range(T):
                act.wait_ge(tr_done, 4 + t + 1)
                nc.scalar.copy(ST[:, t * J:(t + 1) * J], banks[(7, 0)[t]][:]).then_inc(tr_copied, 1)
                nc.scalar.activation(SQ[:, t * J:(t + 1) * J], banks[(7, 0)[t]][:], ACT.Square).then_inc(sq_done, 1)
            for b in range(T):
                act.wait_ge(d2_done, b + 1)
                nc.scalar.activation(D[:, b, :], D[:, b, :], ACT.Sqrt).then_inc(d_done, 1)
            act.wait_ge(gwc_done, 1)
            nc.scalar.copy(carry[:, P:], banks[4][:, 0:NE]).then_inc(gwc_copied, 1)
            for t in range(T):
                act.wait_ge(tr_done, 7 + t)
                nc.scalar.copy(X1T[:, t * J:(t + 1) * J], banks[(7, 0)[t]][:]).then_inc(tr_copied, 1)
            act.wait_ge(ctxg_done, 1)
            act.wait_ge(ctxb_clear, 1)
            for b in range(T):
                nc.scalar.copy(ctxb[32 * b:32 * b + NB, :, P:],
                               banks[6][32 * b:32 * b + NB, 0:KB * NE].rearrange("g (r e) -> g r e", e=NE)
                               ).then_inc(ctxg_copied, 1)
            follow_path(act, nc.scalar.copy, 0, picked0)
            act.wait_ge(var_done, 4)
            root(2, slice(0, NT))
            act.wait_ge(lsh_done, 1)
            nc.scalar.activation(lexp[:], lsh[:], ACT.Exp).then_inc(lexp_done, 1)
            for n in range(0, NT, 2):
                nc.scalar.copy(X2[:, n:n + 2, :], banks[2 + n // 2][:, 0:2 * (P + NE)].rearrange(
                    "p (n f) -> p n f", f=P + NE)[:, :, 0:P]).then_inc(x2_done, 1)
            act.wait_ge(moe_in, 64)
            act.wait_ge(expert_done, 1)

            def normalize(k):
                act.wait_ge(gathered[k], 16)
                if k >= 2:
                    act.wait_ge(xt_done, k - 1)
                nc.scalar.activation(XN[:, k % 2, :], XS[:, k, 0:P], ACT.Identity, bias=XS[:, k, P + 1:P + 2],
                                     scale=XS[:, k, P:P + 1]).then_inc(xn_done, 1)

            def copy_weights(k):
                e = expert_of(act, k)
                if k >= 2:
                    act.wait_ge(hid_done, k - 1)
                nc.scalar.copy(W1K[:, k % 2, :], W1[:, bass.ds(e, 1), :].squeeze(1)).then_inc(w1_copied, 1)

            copy_weights(0)
            normalize(0)
            for k in range(SLOT_TILES):
                act.wait_ge(xt_done, k + 1)
                nc.scalar.copy(XT[:, k % 2, :], banks[k % 2][:, 0:P]).then_inc(xt_copied, 1)
                if k + 1 < SLOT_TILES:
                    normalize(k + 1)
                    copy_weights(k + 1)

        @block.tensor
        def _(pe):
            pe.wait_ge(const_done, 1)

            def transposes(src, bank, t):
                for n in range(TPB):
                    i = nc.tensor.transpose(banks[bank][:, n * P:(n + 1) * P], src[:, t * TPB + n, :], ident[:])
                i.then_inc(tr_done, 1)

            def warm(count):
                for _ in range(count):
                    nc.tensor.matmul(banks[0][:, 0:P], ones[:], ones[:], start=True, stop=True)

            def warm_long(count):
                for _ in range(count):
                    nc.tensor.matmul(banks[0][:], ones[:], W1[:, 0, :], start=True, stop=True)

            warm(WARM_START)
            pe.wait_ge(w_in, 16)
            nc.tensor.matmul(banks[7][:, 0:3 * P], center[:], wqkv[:], start=True, stop=True).then_inc(wc_done, 1)
            for t in range(T):
                pe.wait_ge(x_in[t], 16)
                transposes(X, t, t)
            pe.wait_ge(wc_copied, 1)
            for i in range(TPB):
                for m, n in enumerate((i, i + TPB)):
                    if i == 0:
                        pe.wait_ge(tr_copied, m + 1)
                    nc.tensor.matmul(banks[(2 * i + m + 2) % 8][:, 0:3 * P], XTT[:, n * P:(n + 1) * P], wc[:],
                                     start=True, stop=True).then_inc(qkv_done, 1)
            pe.wait_ge(qkv_copied, NT)
            warm(WARM_ATTENTION)
            for t in range(T):
                pe.wait_ge(att_done, t + 1)
                transposes(att, 2 + t, t)
            for t in range(T):
                pe.wait_ge(tr_copied, 3 + t)
                for n in range(TPB):
                    i = nc.tensor.matmul(banks[4 + t][:, n * P:(n + 1) * P],
                                         attT[:, (t * TPB + n) * P:(t * TPB + n + 1) * P], wo[:], start=True, stop=True)
                i.then_inc(proj_done, 1)
            warm(WARM_NORM)
            pe.wait_ge(m2_done, 1)

            def products(t):
                pe.wait_ge(tr_copied, 5 + t)
                nc.tensor.matmul(banks[1 + t][0:ROWS, :], ctxTm2[:, t * ROWS:(t + 1) * ROWS], ST[:, t * J:(t + 1) * J],
                                 start=True, stop=False)

            def squares(t):
                pe.wait_ge(sq_done, t + 1)
                nc.tensor.matmul(banks[1 + t][0:ROWS, :], ones[:, 0:ROWS], SQ[:, t * J:(t + 1) * J],
                                 start=False, stop=True).then_inc(dist_done, 1)

            pe.wait_ge(norm_done, 1)
            transposes(S, 7, 0)
            products(0)
            pe.wait_ge(norm_done, 2)
            transposes(S, 0, 1)
            squares(0)
            products(1)
            squares(1)
            pe.wait_ge(gate_in, 32)
            nc.tensor.matmul(banks[4][:, 0:NE], center[:], gw[:], start=True, stop=True).then_inc(gwc_done, 1)
            pe.wait_ge(gwc_copied, 1)
            pe.wait_ge(tr_copied, 6)
            for t in range(T):
                transposes(X1, (7, 0)[t], t)
            for b in range(T):
                for r in range(KB):
                    i = nc.tensor.matmul(banks[6][32 * b:32 * b + NB, r * NE:(r + 1) * NE], ctxT[:, b, r::KB], carry[:, P:],
                                         start=True, stop=True)
            i.then_inc(ctxg_done, 1)
            pe.wait_ge(d2_done, 2)

            def token_part(n):
                return banks[2 + n // 2][:, n % 2 * (P + NE):(n % 2 + 1) * (P + NE)]

            for n in range(NT):
                pe.wait_ge(tr_copied, 7 + n // TPB)
                nc.tensor.matmul(token_part(n), X1T[:, n * P:(n + 1) * P], carry[:], start=(n % 2 == 0), stop=False)
            pe.wait_ge(picked1, max(NB - 14, 1))
            warm(WARM_PATH)
            pe.wait_ge(parts_done, 1)
            for m, r in enumerate(range(KB - 1, -1, -1)):
                pe.wait_ge(path_done, m + 1)
                for b in range(T):
                    for n in range(TPB):
                        for part in range(3):
                            i = nc.tensor.matmul(token_part(b * TPB + n),
                                                 onpath[32 * b:32 * b + 32, r, n * P:(n + 1) * P],
                                                 ctxb_part[32 * b:32 * b + 32, r, part, :], start=False,
                                                 stop=(m == KB - 1 and n % 2 == 1 and part == 2))
                    if m == KB - 1:
                        i.then_inc(exp2_done, 1)
            pe.wait_ge(moe_in, 64)
            pe.wait_ge(hit_done, 1)
            places = banks[6][:, NT * NE:2 * NT * NE]
            hot = onehot[:].rearrange("p n e -> p (n e)")
            nc.tensor.matmul(places, before[:], hot, start=True, stop=False)
            for n in range(NT - 1):
                i = nc.tensor.matmul(places[:, (n + 1) * NE:], ones_h[:],
                                     onehot[:, n:n + 1, :].to_broadcast([P, NT - 1 - n, NE]),
                                     start=False, stop=(n == NT - 2))
            i.then_inc(count_done, 1)
            for n in range(NT):
                i = nc.tensor.matmul(banks[7][:, 0:NE], ones_h[:], onehot[:, n, :], start=(n == 0), stop=(n == NT - 1))
            i.then_inc(count_done, 1)
            warm_long(WARM_PLACES)
            for n in range(NT):
                pe.wait_ge(placed, max(n + 2, 4))
                i = nc.tensor.matmul(banks[1][:, 0:2 * SLOT_TILES], at_slot[:, n, :],
                                     number[:, n].rearrange("p k q -> p (k q)"), start=(n == 0), stop=(n == NT - 1))
            i.then_inc(listed, 1)

            def turn_input(k):
                pe.wait_ge(xn_done, k + 1)
                if k >= 2:
                    pe.wait_ge(xt_copied, k - 1)
                nc.tensor.transpose(banks[k % 2][:, 0:P], XN[:, k % 2, :], ident[:]).then_inc(xt_done, 1)

            def hidden(k):
                pe.wait_ge(w1_copied, k + 1)
                pe.wait_ge(xt_copied, k + 1)
                if k >= 2:
                    pe.wait_ge(hid_act, k - 1)
                for c in range(HC):
                    i = nc.tensor.matmul(banks[2 + k % 2][:, c * P:(c + 1) * P], W1K[:, k % 2, c * P:(c + 1) * P],
                                         XT[:, k % 2, :], start=True, stop=True)
                i.then_inc(hid_done, 1)

            def output(k):
                e = expert_of(pe, k)
                pe.wait_ge(hid_act, k + 1)
                if k >= 2:
                    pe.wait_ge(ys_done, k - 1)
                for c in range(HC):
                    i = nc.tensor.matmul(banks[6 + k % 2][:, 0:P], HT2[:, k % 2, c * P:(c + 1) * P],
                                         W2[:, bass.ds(e, 1), c, :].squeeze(1), start=(c == 0), stop=(c == HC - 1))
                i.then_inc(y_done, 1)

            pe.wait_ge(expert_done, 1)
            warm(WARM_EXPERTS)
            turn_input(0)
            hidden(0)
            for k in range(SLOT_TILES + 1):
                if k + 1 < SLOT_TILES:
                    turn_input(k + 1)
                if 1 <= k < SLOT_TILES:
                    hidden(k)
                if k >= 1:
                    output(k - 1)


def kernel(x, ctx_1024, L0_attn_qkv_w, L0_attn_qkv_b, L0_attn_out_w, L0_attn_out_b, L0_ffn_gate_w,
           L0_ffn_gate_b, L0_ffn_w1, L0_ffn_b1, L0_ffn_w2, L0_ffn_b2):
    import numpy as np
    import concourse.bacc as bacc
    from concourse import mybir
    from concourse.bass_utils import run_bass_kernel_spmd

    nc = bacc.Bacc("TRN2", target_bir_lowering=False, num_devices=1)
    given = {
        "x": x, "ctx_rows": ctx_1024,
        "ctx_t": np.transpose(np.asarray(ctx_1024), (2, 0, 1)).reshape(128, -1),
        "qkv_wt": np.transpose(np.asarray(L0_attn_qkv_w)), "qkv_b": L0_attn_qkv_b,
        "out_wt": np.transpose(np.asarray(L0_attn_out_w)), "out_b": L0_attn_out_b,
        "gate_w": L0_ffn_gate_w, "gate_b": L0_ffn_gate_b,
        "w1": L0_ffn_w1, "b1_t": np.transpose(np.asarray(L0_ffn_b1).reshape(-1, 128)), "w2": L0_ffn_w2, "b2": L0_ffn_b2,
    }
    arrays, aps = {}, {}
    for name, a in given.items():
        a = np.ascontiguousarray(a)
        arrays["in_" + name] = a
        aps[name] = nc.dram_tensor("in_" + name, a.shape, mybir.dt.from_np(a.dtype), kind="ExternalInput").ap()
    out = nc.dram_tensor("out_0", (2, 512, 128), mybir.dt.float32, kind="ExternalOutput").ap()
    build(nc, out=out, **aps)
    r = run_bass_kernel_spmd(nc, [arrays], core_ids=[0])
    return r.results[0]["out_0"]
```
